# Optimizing a Trainium2 kernel written in Bass

```python
import numpy as np
import jax
import jax.numpy as jnp

def _softmax(x, axis=-1):
    return jax.nn.softmax(x, axis=axis)

def _gelu(x):
    return jax.nn.gelu(x, approximate=True)

def _silu(x):
    return jax.nn.silu(x)

def _sigmoid(x):
    return jax.nn.sigmoid(x)

def _layernorm(x, axis=-1, eps=1e-05):
    m = jnp.mean(x, axis=axis, keepdims=True)
    v = jnp.var(x, axis=axis, keepdims=True)
    return (x - m) / jnp.sqrt(v + eps)

def _scatter_add(tgt, idx, src, axis=0):
    return tgt.at[idx].add(src)

def _segment_sum(src, seg, n):
    return jax.ops.segment_sum(src, seg, n)
kernel_name = 'mk_dlrm_tower_d1_rec_r8_8f5d8a'

def setup_inputs(seed: int=0):
    np.random.seed(seed)
    _w = jnp.asarray

    def _rec_inputs():
        import jax
        import jax.numpy as jnp
        _tk = jax.random.key(seed)
        dense_ctx = jax.random.normal(jax.random.fold_in(_tk, 190), (512, 16), jnp.float32)
        ids = jnp.stack([jax.random.randint(jax.random.fold_in(_tk, 200 + f), (512,), 0, v, jnp.int32) for f, v in enumerate([1000, 1250, 1250, 1250, 125000, 1000, 125000, 125000, 1000, 1250, 1000, 1000, 1000, 1250, 1250, 12500, 1250, 12500, 12500, 1000, 1000, 12500, 1250, 1000, 1250, 1000, 12500, 1000, 1250, 12500, 12500, 1250, 1250, 1000, 1000, 1000, 1250, 1250, 1000, 1250])], axis=1)
        tbl_0 = 0.05 * jax.random.normal(jax.random.fold_in(_tk, 500 + 0), (1000, 64), jnp.float32)
        tbl_1 = 0.05 * jax.random.normal(jax.random.fold_in(_tk, 500 + 1), (1250, 64), jnp.float32)
        tbl_2 = 0.05 * jax.random.normal(jax.random.fold_in(_tk, 500 + 2), (1250, 64), jnp.float32)
        tbl_3 = 0.05 * jax.random.normal(jax.random.fold_in(_tk, 500 + 3), (1250, 64), jnp.float32)
        tbl_4 = 0.05 * jax.random.normal(jax.random.fold_in(_tk, 500 + 4), (125000, 64), jnp.float32)
        tbl_5 = 0.05 * jax.random.normal(jax.random.fold_in(_tk, 500 + 5), (1000, 64), jnp.float32)
        tbl_6 = 0.05 * jax.random.normal(jax.random.fold_in(_tk, 500 + 6), (125000, 64), jnp.float32)
        tbl_7 = 0.05 * jax.random.normal(jax.random.fold_in(_tk, 500 + 7), (125000, 64), jnp.float32)
        tbl_8 = 0.05 * jax.random.normal(jax.random.fold_in(_tk, 500 + 8), (1000, 64), jnp.float32)
        tbl_9 = 0.05 * jax.random.normal(jax.random.fold_in(_tk, 500 + 9), (1250, 64), jnp.float32)
        tbl_10 = 0.05 * jax.random.normal(jax.random.fold_in(_tk, 500 + 10), (1000, 64), jnp.float32)
        tbl_11 = 0.05 * jax.random.normal(jax.random.fold_in(_tk, 500 + 11), (1000, 64), jnp.float32)
        tbl_12 = 0.05 * jax.random.normal(jax.random.fold_in(_tk, 500 + 12), (1000, 64), jnp.float32)
        tbl_13 = 0.05 * jax.random.normal(jax.random.fold_in(_tk, 500 + 13), (1250, 64), jnp.float32)
        tbl_14 = 0.05 * jax.random.normal(jax.random.fold_in(_tk, 500 + 14), (1250, 64), jnp.float32)
        tbl_15 = 0.05 * jax.random.normal(jax.random.fold_in(_tk, 500 + 15), (12500, 64), jnp.float32)
        tbl_16 = 0.05 * jax.random.normal(jax.random.fold_in(_tk, 500 + 16), (1250, 64), jnp.float32)
        tbl_17 = 0.05 * jax.random.normal(jax.random.fold_in(_tk, 500 + 17), (12500, 64), jnp.float32)
        tbl_18 = 0.05 * jax.random.normal(jax.random.fold_in(_tk, 500 + 18), (12500, 64), jnp.float32)
        tbl_19 = 0.05 * jax.random.normal(jax.random.fold_in(_tk, 500 + 19), (1000, 64), jnp.float32)
        tbl_20 = 0.05 * jax.random.normal(jax.random.fold_in(_tk, 500 + 20), (1000, 64), jnp.float32)
        tbl_21 = 0.05 * jax.random.normal(jax.random.fold_in(_tk, 500 + 21), (12500, 64), jnp.float32)
        tbl_22 = 0.05 * jax.random.normal(jax.random.fold_in(_tk, 500 + 22), (1250, 64), jnp.float32)
        tbl_23 = 0.05 * jax.random.normal(jax.random.fold_in(_tk, 500 + 23), (1000, 64), jnp.float32)
        tbl_24 = 0.05 * jax.random.normal(jax.random.fold_in(_tk, 500 + 24), (1250, 64), jnp.float32)
        tbl_25 = 0.05 * jax.random.normal(jax.random.fold_in(_tk, 500 + 25), (1000, 64), jnp.float32)
        tbl_26 = 0.05 * jax.random.normal(jax.random.fold_in(_tk, 500 + 26), (12500, 64), jnp.float32)
        tbl_27 = 0.05 * jax.random.normal(jax.random.fold_in(_tk, 500 + 27), (1000, 64), jnp.float32)
        tbl_28 = 0.05 * jax.random.normal(jax.random.fold_in(_tk, 500 + 28), (1250, 64), jnp.float32)
        tbl_29 = 0.05 * jax.random.normal(jax.random.fold_in(_tk, 500 + 29), (12500, 64), jnp.float32)
        tbl_30 = 0.05 * jax.random.normal(jax.random.fold_in(_tk, 500 + 30), (12500, 64), jnp.float32)
        tbl_31 = 0.05 * jax.random.normal(jax.random.fold_in(_tk, 500 + 31), (1250, 64), jnp.float32)
        tbl_32 = 0.05 * jax.random.normal(jax.random.fold_in(_tk, 500 + 32), (1250, 64), jnp.float32)
        tbl_33 = 0.05 * jax.random.normal(jax.random.fold_in(_tk, 500 + 33), (1000, 64), jnp.float32)
        tbl_34 = 0.05 * jax.random.normal(jax.random.fold_in(_tk, 500 + 34), (1000, 64), jnp.float32)
        tbl_35 = 0.05 * jax.random.normal(jax.random.fold_in(_tk, 500 + 35), (1000, 64), jnp.float32)
        tbl_36 = 0.05 * jax.random.normal(jax.random.fold_in(_tk, 500 + 36), (1250, 64), jnp.float32)
        tbl_37 = 0.05 * jax.random.normal(jax.random.fold_in(_tk, 500 + 37), (1250, 64), jnp.float32)
        tbl_38 = 0.05 * jax.random.normal(jax.random.fold_in(_tk, 500 + 38), (1000, 64), jnp.float32)
        tbl_39 = 0.05 * jax.random.normal(jax.random.fold_in(_tk, 500 + 39), (1250, 64), jnp.float32)
        _rk = jax.random.fold_in(_tk, 7)
        W_top1 = 0.0354441 * jax.random.normal(jax.random.fold_in(_tk, 801), (796, 512), jnp.float32)
        W_top2 = 0.0441942 * jax.random.normal(jax.random.fold_in(_tk, 802), (512, 256), jnp.float32)
        W_top3 = 0.0625 * jax.random.normal(jax.random.fold_in(_tk, 803), (256, 1), jnp.float32)
        b_top1 = jnp.zeros((512,), jnp.float32)
        b_top2 = jnp.zeros((256,), jnp.float32)
        return (dense_ctx, ids, tbl_0, tbl_1, tbl_2, tbl_3, tbl_4, tbl_5, tbl_6, tbl_7, tbl_8, tbl_9, tbl_10, tbl_11, tbl_12, tbl_13, tbl_14, tbl_15, tbl_16, tbl_17, tbl_18, tbl_19, tbl_20, tbl_21, tbl_22, tbl_23, tbl_24, tbl_25, tbl_26, tbl_27, tbl_28, tbl_29, tbl_30, tbl_31, tbl_32, tbl_33, tbl_34, tbl_35, tbl_36, tbl_37, tbl_38, tbl_39, W_top1, b_top1, W_top2, b_top2, W_top3)
    dense_ctx, ids, tbl_0, tbl_1, tbl_2, tbl_3, tbl_4, tbl_5, tbl_6, tbl_7, tbl_8, tbl_9, tbl_10, tbl_11, tbl_12, tbl_13, tbl_14, tbl_15, tbl_16, tbl_17, tbl_18, tbl_19, tbl_20, tbl_21, tbl_22, tbl_23, tbl_24, tbl_25, tbl_26, tbl_27, tbl_28, tbl_29, tbl_30, tbl_31, tbl_32, tbl_33, tbl_34, tbl_35, tbl_36, tbl_37, tbl_38, tbl_39, W_top1, b_top1, W_top2, b_top2, W_top3 = _rec_inputs()

    def _L0_rec_setup():
        import jax, jax.numpy as jnp
        import numpy as np
        B, N, E = (1024, 40, 64)
        P = N * (N - 1) // 2

        def _pair_indices(n):
            row, col = ([], [])
            for i in range(n - 1):
                for j in range(i + 1, n):
                    row.append(i)
                    col.append(j)
            return (np.asarray(row), np.asarray(col))
        key = jax.random.key(seed)
        k1, k2 = jax.random.split(key)
        inputs = jax.random.normal(k1, (B, N, E), dtype=jnp.float32)
        std = float(np.sqrt(2.0 / (E + E)))
        param = jax.random.normal(k2, (E, P, E), dtype=jnp.float32) * std
        return {'inputs': inputs, 'param': param}
    _L0_rec_all = _L0_rec_setup()
    _L0_rec_in = {k: v for k, v in _L0_rec_all.items() if k in ('param',)}
    del _L0_rec_all
    return {'dense_ctx': dense_ctx, 'ids': ids, 'tbl_0': tbl_0, 'tbl_1': tbl_1, 'tbl_2': tbl_2, 'tbl_3': tbl_3, 'tbl_4': tbl_4, 'tbl_5': tbl_5, 'tbl_6': tbl_6, 'tbl_7': tbl_7, 'tbl_8': tbl_8, 'tbl_9': tbl_9, 'tbl_10': tbl_10, 'tbl_11': tbl_11, 'tbl_12': tbl_12, 'tbl_13': tbl_13, 'tbl_14': tbl_14, 'tbl_15': tbl_15, 'tbl_16': tbl_16, 'tbl_17': tbl_17, 'tbl_18': tbl_18, 'tbl_19': tbl_19, 'tbl_20': tbl_20, 'tbl_21': tbl_21, 'tbl_22': tbl_22, 'tbl_23': tbl_23, 'tbl_24': tbl_24, 'tbl_25': tbl_25, 'tbl_26': tbl_26, 'tbl_27': tbl_27, 'tbl_28': tbl_28, 'tbl_29': tbl_29, 'tbl_30': tbl_30, 'tbl_31': tbl_31, 'tbl_32': tbl_32, 'tbl_33': tbl_33, 'tbl_34': tbl_34, 'tbl_35': tbl_35, 'tbl_36': tbl_36, 'tbl_37': tbl_37, 'tbl_38': tbl_38, 'tbl_39': tbl_39, 'W_top1': W_top1, 'b_top1': b_top1, 'W_top2': W_top2, 'b_top2': b_top2, 'W_top3': W_top3, 'L0_rec_param': _L0_rec_in['param']}

def reference(dense_ctx, ids, tbl_0, tbl_1, tbl_2, tbl_3, tbl_4, tbl_5, tbl_6, tbl_7, tbl_8, tbl_9, tbl_10, tbl_11, tbl_12, tbl_13, tbl_14, tbl_15, tbl_16, tbl_17, tbl_18, tbl_19, tbl_20, tbl_21, tbl_22, tbl_23, tbl_24, tbl_25, tbl_26, tbl_27, tbl_28, tbl_29, tbl_30, tbl_31, tbl_32, tbl_33, tbl_34, tbl_35, tbl_36, tbl_37, tbl_38, tbl_39, W_top1, b_top1, W_top2, b_top2, W_top3, L0_rec_param):
    import jax
    import jax.numpy as jnp

    def _L0_rec_ref(inputs, param):
        import jax, jax.numpy as jnp
        import numpy as np
        B, N, E = (1024, 40, 64)
        P = N * (N - 1) // 2

        def _pair_indices(n):
            row, col = ([], [])
            for i in range(n - 1):
                for j in range(i + 1, n):
                    row.append(i)
                    col.append(j)
            return (np.asarray(row), np.asarray(col))
        n = inputs.shape[1]
        rowidx, colidx = _pair_indices(n)
        p = inputs[:, rowidx]
        q = inputs[:, colidx]
        out = jnp.einsum('bie,fie,bif->bi', p, param, q)
        return out[:, None, :]
    e = jnp.stack([tbl_0[ids[:, 0]], tbl_1[ids[:, 1]], tbl_2[ids[:, 2]], tbl_3[ids[:, 3]], tbl_4[ids[:, 4]], tbl_5[ids[:, 5]], tbl_6[ids[:, 6]], tbl_7[ids[:, 7]], tbl_8[ids[:, 8]], tbl_9[ids[:, 9]], tbl_10[ids[:, 10]], tbl_11[ids[:, 11]], tbl_12[ids[:, 12]], tbl_13[ids[:, 13]], tbl_14[ids[:, 14]], tbl_15[ids[:, 15]], tbl_16[ids[:, 16]], tbl_17[ids[:, 17]], tbl_18[ids[:, 18]], tbl_19[ids[:, 19]], tbl_20[ids[:, 20]], tbl_21[ids[:, 21]], tbl_22[ids[:, 22]], tbl_23[ids[:, 23]], tbl_24[ids[:, 24]], tbl_25[ids[:, 25]], tbl_26[ids[:, 26]], tbl_27[ids[:, 27]], tbl_28[ids[:, 28]], tbl_29[ids[:, 29]], tbl_30[ids[:, 30]], tbl_31[ids[:, 31]], tbl_32[ids[:, 32]], tbl_33[ids[:, 33]], tbl_34[ids[:, 34]], tbl_35[ids[:, 35]], tbl_36[ids[:, 36]], tbl_37[ids[:, 37]], tbl_38[ids[:, 38]], tbl_39[ids[:, 39]]], axis=1)
    z = _L0_rec_ref(e, L0_rec_param)
    z = z.reshape(z.shape[0], -1)
    h = jnp.concatenate([z, dense_ctx], axis=1)
    h = jnp.maximum(h @ W_top1 + b_top1, 0.0)
    h = jnp.maximum(h @ W_top2 + b_top2, 0.0)
    y = h @ W_top3
    return y

_drawn_inputs = setup_inputs


def setup_inputs(seed=0):
    import zlib

    import numpy as np

    out = dict(_drawn_inputs(seed))
    spreads = {'b_top1': (0.0, 0.1), 'b_top2': (0.0, 0.1)}
    factors = {}
    for name, (base, spread) in spreads.items():
        noise = np.random.default_rng([zlib.crc32(name.encode()), seed]).standard_normal(out[name].shape)
        drawn = base * np.exp(spread * noise) if base else spread * noise
        out[name] = jnp.asarray(drawn.astype(out[name].dtype))
    for name, factor in factors.items():
        out[name] = (out[name] * factor).astype(out[name].dtype)
    return out
```

```python
from contextlib import ExitStack

import concourse.bass as bass
from concourse import mybir

P = 128
BATCH = 512
TABLES = 40
EMB = 64
DENSE = 16
HID1 = 512
HID2 = 256

BLOCKS = TABLES // 2
ROWBLKS = BATCH // P
QUAD = 32

F32 = mybir.dt.float32
F32R = mybir.dt.float32r
I32 = mybir.dt.int32
ALU = mybir.AluOpType
ACT = mybir.ActivationFunctionType


def plan_steps():
    steps, ends = [], []
    for m in range(BLOCKS):
        steps += [("cross", m, j) for j in range(m)]
        if m % 2:
            steps.append(("diag", m - 1, m))
        ends.append(len(steps))
    return steps, ends


def tile_pairs():
    tiles = []
    for kind, m, j in plan_steps()[0]:
        if kind == "cross":
            tiles += [((2 * j, c), (2 * j + 1, c)) for c in (2 * m, 2 * m + 1)]
        else:
            tiles += [((2 * k, 2 * k + 1), None) for k in (m, j)]
    return tiles


STEPS, BLOCK_END = plan_steps()
NSTEPS = len(STEPS)
CHUNK = 5
CHUNKS = NSTEPS // CHUNK
BATCH_STEPS = 2
ZTILES = 2 * P // QUAD * QUAD // 4
ZSTEPS = ZTILES // 2
ZCHUNKS = -(-NSTEPS // ZSTEPS)
DENSE_ROW = 8


def z_row(tile, odd):
    chunk, at = divmod(tile, ZTILES)
    return chunk * P + (at % 4) * QUAD + 2 * (at // 4) + odd


RAW_SLOTS = 2
W_SLOTS = 3
X_SLOTS = 3
V_SLOTS = 3
PROD_SLOTS = 6
BLOCK_LEAD = 8
ROW_SLOTS = 4


def block_prep_at():
    at = {0: [0, 1]}
    for m in range(1, BLOCKS - 1):
        at.setdefault(max(BLOCK_END[m - 1], BLOCK_END[m] - BLOCK_LEAD), []).append(m + 1)
    return at


def chunk_prep_at():
    at = {0: [0, 1]}
    for k in range(2, CHUNKS):
        at.setdefault(CHUNK * (k - 2) + 1, []).append(k)
    return at


def dlrm_tower(nc, dense_t, ids, tables, weights, w1, b1, w2, b2, w3, ident_in, out):
    assert NSTEPS % CHUNK == 0 and NSTEPS % BATCH_STEPS == 0
    prep_block, prep_chunk = block_prep_at(), chunk_prep_at()
    K1 = ZCHUNKS
    K2 = HID1 // P
    K3 = HID2 // P
    SPLIT_MLP_AT = 2 * NSTEPS // 3
    SPLIT_MLP_EVERY = 5

    with ExitStack() as ctx:
        def sb(name, shape, dt):
            return ctx.enter_context(nc.sbuf_tensor(name, shape, dt))

        def sem(name):
            return ctx.enter_context(nc.semaphore(name))

        ident = sb("ident", [P, P + 2 * QUAD], F32)
        selector = sb("selector", [P, 2 * QUAD], F32)
        ids_sb = sb("ids_sb", [P, ROWBLKS, TABLES], I32)
        rows = sb("rows", [P, ROW_SLOTS, ROWBLKS, 2, EMB], F32)
        x_t = sb("x_t", [P, BLOCKS, BATCH], F32)
        x_split = sb("x_split", [P, 2, 2, BATCH], F32R)
        x_dup = sb("x_dup", [P, X_SLOTS, 2, 2, BATCH], F32R)
        raw = sb("raw", [P, RAW_SLOTS, CHUNK * P], F32)
        w_high = sb("w_high", [P, 2, CHUNK * P], F32R)
        w_low = sb("w_low", [P, 2, CHUNK * P], F32R)
        w_st = sb("w_st", [P, W_SLOTS, 2, CHUNK * P], F32R)
        prod = sb("prod", [P, PROD_SLOTS, 2, BATCH], F32)
        z_high = sb("z_high", [P, K1, BATCH], F32R)
        z_low = sb("z_low", [P, K1, BATCH], F32R)
        w3_sb = sb("w3_sb", [P, K3], F32)
        b1_sb = sb("b1_sb", [P, K2], F32)
        b2_sb = sb("b2_sb", [P, K3], F32)
        dense_sb = sb("dense_sb", [DENSE, BATCH], F32)
        w1_raw = sb("w1_raw", [P, HID1], F32)
        w1_high = sb("w1_high", [P, K1, HID1], F32R)
        w1_low = sb("w1_low", [P, K1, HID1], F32R)
        w2_raw = sb("w2_raw", [P, HID2], F32)
        w2_high = sb("w2_high", [P, K2, HID2], F32R)
        w2_low = sb("w2_low", [P, K2, HID2], F32R)
        h1 = prod[:, 0:2, :, :].rearrange("p a b n -> p (a b) n")
        h1_high = x_dup[:, 0, :, :, :].rearrange("p a b n -> p (a b) n")
        h1_low = x_dup[:, 1, :, :, :].rearrange("p a b n -> p (a b) n")
        h2 = prod[:, 4, :, :]
        y_sb = prod[0:1, 5, 0, :]

        v_ps = ctx.enter_context(nc.psum_tensor("v_ps", [P, V_SLOTS, 2, BATCH], F32))
        z_ps = ctx.enter_context(nc.psum_tensor("z_ps", [P, BATCH], F32))
        t_ps = ctx.enter_context(nc.psum_tensor("t_ps", [P, BATCH], F32))
        h1_ps = v_ps[:, 0:2, :, :].rearrange("p a b n -> p (a b) n")
        h2_ps = v_ps[:, 2, :, :]
        y_ps = t_ps[0:1, :]

        consts_loaded = sem("consts_loaded")
        ids_loaded = sem("ids_loaded")
        mlp_loaded = sem("mlp_loaded")
        w1_loaded = sem("w1_loaded")
        w2_loaded = sem("w2_loaded")
        gathered = [sem(f"gathered{m}") for m in range(BLOCKS)]
        transposed = sem("transposed")
        x_copied = sem("x_copied")
        x_low_done = sem("x_low_done")
        x_dup_moved = [sem(f"x_dup_moved{i}") for i in range(X_SLOTS)]
        raw_loaded = [sem(f"raw_loaded{i}") for i in range(RAW_SLOTS)]
        w_high_done = sem("w_high_done")
        w_st_high = sem("w_st_high")
        w_low_done = sem("w_low_done")
        w_low_moved = [sem(f"w_low_moved{i}") for i in range(W_SLOTS)]
        v_done = sem("v_done")
        prod_done = sem("prod_done")
        reduced = sem("reduced")
        z_high_done = sem("z_high_done")
        z_low_done = sem("z_low_done")
        w1_high_done = sem("w1_high_done")
        w1_low_done = sem("w1_low_done")
        w2_high_done = sem("w2_high_done")
        w2_low_done = sem("w2_low_done")
        h1_summed = sem("h1_summed")
        h1_done = sem("h1_done")
        h1_high_done = sem("h1_high_done")
        h1_low_done = sem("h1_low_done")
        h2_summed = sem("h2_summed")
        h2_done = sem("h2_done")
        y_summed = sem("y_summed")
        y_done = sem("y_done")
        y_stored = sem("y_stored")

        block = ctx.enter_context(nc.Block())

        def selector_at(tile):
            first = QUAD - 1 - 2 * (tile % ZTILES // 4)
            return selector[:, first:first + QUAD]

        def blocks_before(t):
            return sum(len(v) for at, v in prep_block.items() if at <= t)

        @block.sync
        def _(sp):
            sp.dma_start(ids_sb[:, :, :], ids.rearrange("(k p) c -> p k c", p=P)).then_inc(ids_loaded, 16)
            sp.dma_start(ident[:, :], ident_in[:, 0:P + 2 * QUAD]).then_inc(consts_loaded, 16)
            sp.dma_start(selector[:, :], ident_in[:, P + 2 * QUAD:]).then_inc(consts_loaded, 16)
            sp.dma_start(dense_sb[:, :], dense_t).then_inc(consts_loaded, 16)

            def load_raw(k):
                if k >= RAW_SLOTS:
                    sp.wait_ge(w_high_done, k - RAW_SLOTS + 1)
                    sp.wait_ge(w_st_high, 2 * (k - RAW_SLOTS + 1))
                    sp.wait_ge(w_low_done, k - RAW_SLOTS + 1)
                sp.dma_start(raw[:, k % RAW_SLOTS, :], weights[:, k * CHUNK * P:(k + 1) * CHUNK * P]) \
                    .then_inc(raw_loaded[k % RAW_SLOTS], 16)

            def move_low(k):
                sp.wait_ge(w_low_done, k + 1)
                if k >= W_SLOTS:
                    sp.wait_ge(v_done, CHUNK * (k - W_SLOTS + 1))
                sp.dma_start(w_st[EMB:P, k % W_SLOTS, 0, :].bitcast(F32), w_low[0:EMB, k % 2, :].bitcast(F32)) \
                    .then_inc(w_low_moved[k % W_SLOTS], 16)
                sp.dma_start(w_st[0:EMB, k % W_SLOTS, 1, :].bitcast(F32), w_low[EMB:P, k % 2, :].bitcast(F32)) \
                    .then_inc(w_low_moved[k % W_SLOTS], 16)

            def duplicate(m):
                sp.wait_ge(x_copied, 2 * (m + 1))
                sp.wait_ge(x_low_done, m + 1)
                if m >= X_SLOTS:
                    sp.wait_ge(v_done, BLOCK_END[(m - X_SLOTS) | 1])
                for half in range(2):
                    for table in range(2):
                        sp.dma_start(x_dup[half * EMB:(half + 1) * EMB, m % X_SLOTS, table, :, :].bitcast(F32),
                                     x_split[table * EMB:(table + 1) * EMB, m % 2, :, :].bitcast(F32)) \
                            .then_inc(x_dup_moved[m % X_SLOTS], 16)

            for k in range(RAW_SLOTS):
                load_raw(k)
            for t in range(NSTEPS):
                for k in prep_chunk.get(t, []):
                    move_low(k)
                    if k + 1 >= RAW_SLOTS and k + 1 < CHUNKS:
                        load_raw(k + 1)
                for m in prep_block.get(t, []):
                    duplicate(m)
                if t == CHUNK:
                    sp.dma_start(b1_sb[:, :], b1).then_inc(mlp_loaded, 16)
                    sp.dma_start(b2_sb[:, :], b2).then_inc(mlp_loaded, 16)
                    sp.dma_start(w3_sb[:, :], w3).then_inc(mlp_loaded, 16)
            sp.wait_ge(y_done, 1)
            sp.dma_start(out, y_sb).then_inc(y_stored, 16)
            sp.wait_ge(y_stored, 16)

        @block.gpsimd
        def _(pool):
            def split_mlp_weights():
                for k in range(K1):
                    if k >= 1:
                        pool.wait_ge(w1_low_done, k)
                    nc.gpsimd.dma_start(w1_raw[:, :], w1[k * P:(k + 1) * P, :]).then_inc(w1_loaded, 16)
                    pool.wait_ge(w1_high_done, k + 1)
                    nc.gpsimd.tensor_tensor(w1_low[:, k, :], w1_raw[:, :], w1_high[:, k, :],
                                            ALU.subtract).then_inc(w1_low_done, 1)
                for k in range(K2):
                    if k >= 1:
                        pool.wait_ge(w2_low_done, k)
                    nc.gpsimd.dma_start(w2_raw[:, :], w2[k * P:(k + 1) * P, :]).then_inc(w2_loaded, 16)
                    pool.wait_ge(w2_high_done, k + 1)
                    nc.gpsimd.tensor_tensor(w2_low[:, k, :], w2_raw[:, :], w2_high[:, k, :],
                                            ALU.subtract).then_inc(w2_low_done, 1)

            pool.wait_ge(ids_loaded, 16)
            for c in range(TABLES):
                m = c // 2
                if c % 2 == 0 and m >= ROW_SLOTS:
                    pool.wait_ge(transposed, m - ROW_SLOTS + 1)
                for k in range(ROWBLKS):
                    pool.indirect_dma_start(
                        rows[:, m % ROW_SLOTS, k, c % 2, :], None, tables[c],
                        bass.IndirectOffsetOnAxis(ap=ids_sb[:, k, c:c + 1], axis=0),
                    ).then_inc(gathered[m], 16)
            split_mlp_weights()

        @block.scalar
        def _(act):
            def split_chunk(k):
                act.wait_ge(raw_loaded[k % RAW_SLOTS], 16 * (k // RAW_SLOTS + 1))
                if k >= 2:
                    act.wait_ge(w_low_done, k - 1)
                nc.scalar.activation(w_high[:, k % 2, :], raw[:, k % RAW_SLOTS, :], ACT.Copy) \
                    .then_inc(w_high_done, 1)
                if k >= W_SLOTS:
                    act.wait_ge(v_done, CHUNK * (k - W_SLOTS + 1))
                for tile in range(2):
                    half = slice(tile * EMB, (tile + 1) * EMB)
                    nc.scalar.activation(w_st[half, k % W_SLOTS, tile, :], raw[half, k % RAW_SLOTS, :],
                                         ACT.Copy).then_inc(w_st_high, 1)

            def copy_block(m):
                act.wait_ge(transposed, m + 1)
                nc.scalar.activation(x_t[:, m, :], t_ps[:, :], ACT.Copy).then_inc(x_copied, 1)
                if m >= 2:
                    act.wait_ge(x_dup_moved[(m - 2) % X_SLOTS], 64 * ((m - 2) // X_SLOTS + 1))
                    act.wait_ge(x_low_done, m - 1)
                nc.scalar.activation(x_split[:, m % 2, 0, :], t_ps[:, :], ACT.Copy).then_inc(x_copied, 1)

            def z_chunk(n):
                act.wait_ge(reduced, min((n + 1) * ZSTEPS, NSTEPS) // BATCH_STEPS)
                nc.scalar.activation(z_high[:, n, :], z_ps[:, :], ACT.Copy).then_inc(z_high_done, 1)

            for t in range(NSTEPS):
                for k in prep_chunk.get(t, []):
                    split_chunk(k)
                for m in prep_block.get(t, []):
                    copy_block(m)
                if t >= ZSTEPS + 4 and (t - 4) % ZSTEPS == 0:
                    z_chunk((t - 4) // ZSTEPS - 1)
                k, rest = divmod(t - SPLIT_MLP_AT, SPLIT_MLP_EVERY)
                if rest == 0 and 0 <= k < K1:
                    act.wait_ge(w1_loaded, 16 * (k + 1))
                    nc.scalar.activation(w1_high[:, k, :], w1_raw[:, :], ACT.Copy).then_inc(w1_high_done, 1)
                k -= K1
                if rest == 0 and 0 <= k < K2:
                    act.wait_ge(w2_loaded, 16 * (k + 1))
                    nc.scalar.activation(w2_high[:, k, :], w2_raw[:, :], ACT.Copy).then_inc(w2_high_done, 1)
            z_chunk(ZCHUNKS - 1)

            act.wait_ge(mlp_loaded, 48)
            for i in range(K2):
                act.wait_ge(h1_summed, i + 1)
                nc.scalar.activation(h1[:, i, :], h1_ps[:, i, :], ACT.Relu, bias=b1_sb[:, i:i + 1]) \
                    .then_inc(h1_done, 1)
                nc.scalar.activation(h1_high[:, i, :], h1_ps[:, i, :], ACT.Relu, bias=b1_sb[:, i:i + 1]) \
                    .then_inc(h1_high_done, 1)
            for i in range(K3):
                act.wait_ge(h2_summed, i + 1)
                nc.scalar.activation(h2[:, i, :], h2_ps[:, i, :], ACT.Relu, bias=b2_sb[:, i:i + 1]) \
                    .then_inc(h2_done, 1)
            act.wait_ge(y_summed, 1)
            nc.scalar.activation(y_sb, y_ps, ACT.Copy).then_inc(y_done, 1)

        @block.vector
        def _(dve):
            def low_chunk(k):
                dve.wait_ge(w_high_done, k + 1)
                if k >= 2:
                    dve.wait_ge(w_low_moved[(k - 2) % W_SLOTS], 32 * ((k - 2) // W_SLOTS + 1))
                nc.vector.tensor_tensor(w_low[:, k % 2, :], raw[:, k % RAW_SLOTS, :], w_high[:, k % 2, :],
                                        ALU.subtract).then_inc(w_low_done, 1)

            def low_block(m):
                dve.wait_ge(x_copied, 2 * (m + 1))
                if m >= 2:
                    dve.wait_ge(x_dup_moved[(m - 2) % X_SLOTS], 64 * ((m - 2) // X_SLOTS + 1))
                nc.vector.tensor_tensor(x_split[:, m % 2, 1, :], x_t[:, m, :], x_split[:, m % 2, 0, :],
                                        ALU.subtract).then_inc(x_low_done, 1)

            def z_chunk(n):
                dve.wait_ge(z_high_done, n + 1)
                nc.vector.tensor_tensor(z_low[:, n, :], z_ps[:, :], z_high[:, n, :], ALU.subtract) \
                    .then_inc(z_low_done, 1)

            def multiply(t):
                kind, m, j = STEPS[t]
                dve.wait_ge(v_done, t + 1)
                if t >= PROD_SLOTS:
                    dve.wait_ge(reduced, (t - PROD_SLOTS) // BATCH_STEPS + 1)
                if kind == "cross":
                    x = x_t[:, j, :].unsqueeze(1).to_broadcast([P, 2, BATCH])
                else:
                    x = x_t[:, m:m + 2, :]
                nc.vector.tensor_tensor(prod[:, t % PROD_SLOTS, :, :], v_ps[:, t % V_SLOTS, :, :], x,
                                        ALU.mult).then_inc(prod_done, 1)

            for t in range(NSTEPS):
                for k in prep_chunk.get(t, []):
                    low_chunk(k)
                for m in prep_block.get(t, []):
                    low_block(m)
                if t >= ZSTEPS + 4 and (t - 4) % ZSTEPS == 0:
                    z_chunk((t - 4) // ZSTEPS - 1)
                multiply(t)
            z_chunk(ZCHUNKS - 1)
            for i in range(K2):
                dve.wait_ge(h1_done, i + 1)
                dve.wait_ge(h1_high_done, i + 1)
                nc.vector.tensor_tensor(h1_low[:, i, :], h1[:, i, :], h1_high[:, i, :], ALU.subtract) \
                    .then_inc(h1_low_done, 1)

        @block.tensor
        def _(pe):
            def transpose_block(m):
                pe.wait_ge(gathered[m], 16 * 2 * ROWBLKS)
                if m >= 1:
                    pe.wait_ge(x_copied, 2 * m)
                for k in range(ROWBLKS):
                    last = nc.tensor.transpose(
                        t_ps[:, k * P:(k + 1) * P],
                        rows[:, m % ROW_SLOTS, k, :, :].rearrange("p c e -> p (c e)"),
                        ident[:, QUAD:QUAD + P])
                last.then_inc(transposed, 1)

            def bilinear(t):
                kind, m, j = STEPS[t]
                k, at = divmod(t, CHUNK)
                if at == 0:
                    pe.wait_ge(w_st_high, 2 * (k + 1))
                    pe.wait_ge(w_low_moved[k % W_SLOTS], 32 * (k // W_SLOTS + 1))
                newest = max(m, j)
                pe.wait_ge(x_dup_moved[newest % X_SLOTS], 64 * (newest // X_SLOTS + 1))
                if t >= V_SLOTS:
                    pe.wait_ge(prod_done, t - V_SLOTS + 1)
                for tile in range(2):
                    blk, table = (m, tile) if kind == "cross" else ((m, j)[tile], 1)
                    for part in range(2):
                        last = nc.tensor.matmul(
                            v_ps[:, t % V_SLOTS, tile, :],
                            w_st[:, k % W_SLOTS, tile, at * P:(at + 1) * P],
                            x_dup[:, blk % X_SLOTS, table, part, :],
                            start=(part == 0), stop=(part == 1))
                last.then_inc(v_done, 1)

            def reduce_batch(n):
                t0 = n * BATCH_STEPS
                chunk = t0 // ZSTEPS
                pe.wait_ge(prod_done, t0 + BATCH_STEPS)
                if t0 % ZSTEPS == 0 and chunk >= 1:
                    pe.wait_ge(z_high_done, chunk)
                    pe.wait_ge(z_low_done, chunk)
                last_of_chunk = t0 % ZSTEPS == ZSTEPS - BATCH_STEPS or t0 == NSTEPS - BATCH_STEPS
                for i in range(2 * BATCH_STEPS):
                    step, tile = t0 + i // 2, 2 * t0 + i
                    quad = tile % 4
                    ends = last_of_chunk and not (quad == 0 and t0 == NSTEPS - BATCH_STEPS)
                    last = nc.tensor.matmul(z_ps[quad * QUAD:(quad + 1) * QUAD, :], selector_at(tile),
                                            prod[:, step % PROD_SLOTS, i % 2, :],
                                            start=(t0 % ZSTEPS == 0), stop=ends)
                if t0 == NSTEPS - BATCH_STEPS:
                    last = nc.tensor.matmul(z_ps[0:QUAD, :],
                                            ident[0:DENSE, QUAD - DENSE_ROW:2 * QUAD - DENSE_ROW],
                                            dense_sb[:, :], start=False, stop=True)
                last.then_inc(reduced, 1)

            pe.wait_ge(consts_loaded, 48)
            for t in range(NSTEPS):
                for m in prep_block.get(t, []):
                    transpose_block(m)
                bilinear(t)
                if t >= V_SLOTS and (t - V_SLOTS) % BATCH_STEPS == BATCH_STEPS - 1:
                    reduce_batch((t - V_SLOTS) // BATCH_STEPS)
            for n in range((NSTEPS - 1 - V_SLOTS - BATCH_STEPS + 1) // BATCH_STEPS + 1, NSTEPS // BATCH_STEPS):
                reduce_batch(n)

            def layer(out_ps, w_hi, w_lo, in_hi, in_lo, chunks, in_ready, summed):
                for n in range(chunks):
                    if in_ready is not None:
                        in_ready(n)
                    for p, (w, x) in enumerate(((w_hi, in_hi), (w_lo, in_hi), (w_hi, in_lo))):
                        last = nc.tensor.matmul(out_ps, w(n), x(n), start=(n == 0 and p == 0),
                                                stop=(n == chunks - 1 and p == 2))
                last.then_inc(summed, 1)

            pe.wait_ge(prod_done, NSTEPS)
            pe.wait_ge(w1_high_done, K1)
            pe.wait_ge(w1_low_done, K1)

            def z_ready(n):
                pe.wait_ge(z_high_done, n + 1)
                pe.wait_ge(z_low_done, n + 1)

            def h1_ready(n):
                pe.wait_ge(h1_high_done, n + 1)
                pe.wait_ge(h1_low_done, n + 1)

            for i in range(K2):
                cols = slice(i * P, (i + 1) * P)
                layer(h1_ps[:, i, :], lambda n: w1_high[:, n, cols], lambda n: w1_low[:, n, cols],
                      lambda n: z_high[:, n, :], lambda n: z_low[:, n, :], K1, z_ready if i == 0 else None,
                      h1_summed)
            pe.wait_ge(w2_high_done, K2)
            pe.wait_ge(w2_low_done, K2)
            for i in range(K3):
                cols = slice(i * P, (i + 1) * P)
                layer(h2_ps[:, i, :], lambda n: w2_high[:, n, cols], lambda n: w2_low[:, n, cols],
                      lambda n: h1_high[:, n, :], lambda n: h1_low[:, n, :], K2, h1_ready if i == 0 else None,
                      h2_summed)
            pe.wait_ge(mlp_loaded, 48)
            pe.wait_ge(x_copied, 2 * BLOCKS)
            for n in range(K3):
                pe.wait_ge(h2_done, n + 1)
                last = nc.tensor.matmul(y_ps, w3_sb[:, n:n + 1], h2[:, n, :], start=(n == 0),
                                        stop=(n == K3 - 1))
            last.then_inc(y_summed, 1)


def kernel(**inputs):
    import numpy as np
    import concourse.bacc as bacc
    from concourse.bass_utils import run_bass_kernel_spmd

    pair_of = {}
    for r in range(TABLES - 1):
        for c in range(r + 1, TABLES):
            pair_of[(r, c)] = len(pair_of)
    tiles = tile_pairs()

    param = np.asarray(inputs["L0_rec_param"])
    npairs = param.shape[1]
    order = np.array([[npairs if rc is None else pair_of[rc] for rc in t] for t in tiles])
    padded = np.concatenate([param, np.zeros((EMB, 1, EMB), param.dtype)], axis=1)
    weights = padded[:, order.reshape(NSTEPS, 2, 2), :]
    weights = np.ascontiguousarray(weights.transpose(2, 0, 1, 3, 4).reshape(P, NSTEPS * P))

    w_top1 = np.asarray(inputs["W_top1"])
    w1 = np.zeros((ZCHUNKS * P, HID1), w_top1.dtype)
    for t, pairs in enumerate(tiles):
        for odd, rc in enumerate(pairs):
            if rc is not None:
                w1[z_row(t, odd)] = w_top1[pair_of[rc]]
    dense_at = (ZCHUNKS - 1) * P + DENSE_ROW
    w1[dense_at:dense_at + DENSE] = w_top1[npairs:]

    consts = np.zeros((P, P + 4 * QUAD), np.float32)
    consts[:, QUAD:QUAD + P] = np.eye(P, dtype=np.float32)
    consts[0:EMB, P + 2 * QUAD + QUAD - 1] = 1.0
    consts[EMB:P, P + 2 * QUAD + QUAD] = 1.0

    arrays = {
        "dense_t": np.ascontiguousarray(np.asarray(inputs["dense_ctx"]).T),
        "ids": np.ascontiguousarray(inputs["ids"]),
        "weights": weights,
        "w1": w1,
        "b1": np.ascontiguousarray(np.asarray(inputs["b_top1"]).reshape(-1, P).T),
        "w2": np.ascontiguousarray(inputs["W_top2"]),
        "b2": np.ascontiguousarray(np.asarray(inputs["b_top2"]).reshape(-1, P).T),
        "w3": np.ascontiguousarray(np.asarray(inputs["W_top3"]).reshape(-1, P).T),
        "consts": consts,
    }
    for c in range(TABLES):
        arrays[f"tbl_{c}"] = np.ascontiguousarray(inputs[f"tbl_{c}"])

    nc = bacc.Bacc("TRN2", target_bir_lowering=False, num_devices=1)
    dram = {name: nc.dram_tensor(name, a.shape, mybir.dt.from_np(a.dtype), kind="ExternalInput").ap()
            for name, a in arrays.items()}
    y = nc.dram_tensor("y", (1, BATCH), F32, kind="ExternalOutput").ap()
    dlrm_tower(nc, dram["dense_t"], dram["ids"], [dram[f"tbl_{c}"] for c in range(TABLES)], dram["weights"],
               dram["w1"], dram["b1"], dram["w2"], dram["b2"], dram["w3"], dram["consts"], y)
    result = run_bass_kernel_spmd(nc, [arrays], core_ids=[0])
    return result.results[0]["y"].reshape(BATCH, 1)
```

```python
from contextlib import ExitStack

import concourse.bass as bass
from concourse import mybir

P = 128
BATCH = 512
TABLES = 40
EMB = 64
DENSE = 16
HID1 = 512
HID2 = 256

BLOCKS = TABLES // 2
ROWBLKS = BATCH // P
QUAD = 32

F32 = mybir.dt.float32
F32R = mybir.dt.float32r
I32 = mybir.dt.int32
ALU = mybir.AluOpType
ACT = mybir.ActivationFunctionType


def plan_steps():
    steps, ends = [], []
    for m in range(BLOCKS):
        steps += [("cross", m, j) for j in range(m)] if m > 1 else [("cross", 0, 1)] * m
        if m % 2:
            steps.append(("diag", m - 1, m))
        ends.append(len(steps))
    return steps, ends


def tile_pairs():
    tiles = []
    for kind, m, j in plan_steps()[0]:
        if kind == "cross":
            tiles += [((2 * j, c), (2 * j + 1, c)) for c in (2 * m, 2 * m + 1)]
        else:
            tiles += [((2 * k, 2 * k + 1), None) for k in (m, j)]
    return tiles


def table_order(rows_of):
    first = [c for c, n in enumerate(rows_of) if n == LOOKUP_ROWS][:2 * LOOKED_UP_BLOCKS]
    assert len(first) == 2 * LOOKED_UP_BLOCKS
    return first + [c for c in range(len(rows_of)) if c not in first]


STEPS, BLOCK_END = plan_steps()
NSTEPS = len(STEPS)
CHUNK = 4
CHUNKS = NSTEPS // CHUNK
BATCH_STEPS = 4
ZTILES = 2 * P // QUAD * QUAD // 4
ZSTEPS = ZTILES // 2
ZCHUNKS = -(-NSTEPS // ZSTEPS)
DENSE_ROW = 8


def z_row(tile, odd):
    chunk, at = divmod(tile, ZTILES)
    return chunk * P + (at % 4) * QUAD + 2 * (at // 4) + odd


RAW_SLOTS = 3
W_SLOTS = 3
X_SLOTS = 3
V_SLOTS = 3
PROD_SLOTS = 8
LOOKED_UP_BLOCKS = 2
LOOKUP_ROWS = 1000
LOOKUP_CHUNKS = 8
LOOKUP_PARTS = LOOKUP_ROWS // LOOKUP_CHUNKS
HOT_SLOTS = 4
BLOCK_LEAD = 10
ROW_SLOTS = 4


def block_prep_at():
    at = {0: [0, 1]}
    for m in range(1, BLOCKS - 1):
        at.setdefault(max(BLOCK_END[m - 1], BLOCK_END[m] - BLOCK_LEAD), []).append(m + 1)
    return at


def chunk_prep_at():
    at = {0: [0, 1]}
    for k in range(2, CHUNKS):
        at.setdefault(CHUNK * (k - 2) + 1, []).append(k)
    return at


def dlrm_tower(nc, dense_t, ids, first_ids, tables, weights, w1, b1, w2, b2, w3, ident_in, row_no_in, out):
    assert NSTEPS % CHUNK == 0 and NSTEPS % BATCH_STEPS == 0
    prep_block, prep_chunk = block_prep_at(), chunk_prep_at()
    K1 = ZCHUNKS
    K2 = HID1 // P
    K3 = HID2 // P
    mlp_parts = [(1, k) for k in range(K1)] + [(2, k) for k in range(K2)]
    split_mlp_at = {2 * NSTEPS // 3 + 5 * i: part for i, part in enumerate(mlp_parts)}

    with ExitStack() as ctx:
        def sb(name, shape, dt):
            return ctx.enter_context(nc.sbuf_tensor(name, shape, dt))

        def sem(name):
            return ctx.enter_context(nc.semaphore(name))

        ident = sb("ident", [P, P + 2 * QUAD], F32)
        selector = sb("selector", [P, 2 * QUAD], F32)
        ids_sb = sb("ids_sb", [P, ROWBLKS, TABLES], I32)
        rows = sb("rows", [P, ROW_SLOTS, ROWBLKS, 2, EMB], F32)
        x_t = sb("x_t", [P, BLOCKS, BATCH], F32)
        x_split = sb("x_split", [P, 2, 2, BATCH], F32R)
        x_dup = sb("x_dup", [P, X_SLOTS, 2, 2, BATCH], F32R)
        raw = sb("raw", [P, RAW_SLOTS, CHUNK * P], F32)
        w_high = sb("w_high", [P, 2, CHUNK * P], F32R)
        w_low = sb("w_low", [P, 2, CHUNK * P], F32R)
        w_st = sb("w_st", [P, W_SLOTS, 2, CHUNK * P], F32R)
        prod = sb("prod", [P, PROD_SLOTS, 2, BATCH], F32)
        z_high = sb("z_high", [P, K1, BATCH], F32R)
        z_low = sb("z_low", [P, K1, BATCH], F32R)
        w3_sb = sb("w3_sb", [P, K3], F32)
        b1_sb = sb("b1_sb", [P, K2], F32)
        b2_sb = sb("b2_sb", [P, K3], F32)
        dense_sb = sb("dense_sb", [DENSE, BATCH], F32)
        row_no = sb("row_no", [P, LOOKUP_CHUNKS], F32)
        w1_raw = sb("w1_raw", [P, HID1], F32)
        w1_high = sb("w1_high", [P, K1, HID1], F32R)
        w1_low = sb("w1_low", [P, K1, HID1], F32R)
        w2_raw = w1_raw[:, 0:HID2]
        w2_high = sb("w2_high", [P, K2, HID2], F32R)
        w2_low = sb("w2_low", [P, K2, HID2], F32R)
        look_ids = prod[:, 0:LOOKED_UP_BLOCKS, :, :].bitcast(I32)
        look_rows = prod[:, LOOKED_UP_BLOCKS:2 * LOOKED_UP_BLOCKS, :, :]
        one_hot = prod[:, 2 * LOOKED_UP_BLOCKS:, :, :].rearrange("p a b n -> p (a b) n")
        assert 2 * LOOKED_UP_BLOCKS + HOT_SLOTS // 2 <= PROD_SLOTS and LOOKUP_CHUNKS * EMB == BATCH
        h1 = prod[:, 0:2, :, :].rearrange("p a b n -> p (a b) n")
        h1_high = x_dup[:, 0, :, :, :].rearrange("p a b n -> p (a b) n")
        h1_low = x_dup[:, 1, :, :, :].rearrange("p a b n -> p (a b) n")
        h2 = prod[:, 4, :, :]
        y_sb = prod[0:1, 5, 0, :]

        v_ps = ctx.enter_context(nc.psum_tensor("v_ps", [P, V_SLOTS, 2, BATCH], F32))
        z_ps = ctx.enter_context(nc.psum_tensor("z_ps", [P, BATCH], F32))
        t_ps = ctx.enter_context(nc.psum_tensor("t_ps", [P, BATCH], F32))
        h1_ps = v_ps[:, 0:2, :, :].rearrange("p a b n -> p (a b) n")
        h2_ps = v_ps[:, 2, :, :]
        y_ps = t_ps[0:1, :]
        look_ps = v_ps[:, V_SLOTS - 1, :, :]

        consts_loaded = sem("consts_loaded")
        ids_loaded = sem("ids_loaded")
        row_no_loaded = sem("row_no_loaded")
        mlp_loaded = sem("mlp_loaded")
        w1_loaded = sem("w1_loaded")
        w2_loaded = sem("w2_loaded")
        look_loaded = [sem(f"look_loaded{m}") for m in range(LOOKED_UP_BLOCKS)]
        one_hot_done = sem("one_hot_done")
        one_hot_used = sem("one_hot_used")
        gathered = [sem(f"gathered{m}") for m in range(BLOCKS)]
        transposed = sem("transposed")
        x_copied = sem("x_copied")
        x_low_done = sem("x_low_done")
        x_dup_moved = [sem(f"x_dup_moved{i}") for i in range(X_SLOTS)]
        raw_loaded = [sem(f"raw_loaded{i}") for i in range(RAW_SLOTS)]
        w_high_done = sem("w_high_done")
        w_st_high = sem("w_st_high")
        w_low_done = sem("w_low_done")
        w_low_moved = [sem(f"w_low_moved{i}") for i in range(W_SLOTS)]
        v_done = sem("v_done")
        prod_done = sem("prod_done")
        reduced = sem("reduced")
        z_high_done = sem("z_high_done")
        z_low_done = sem("z_low_done")
        w1_high_done = sem("w1_high_done")
        w1_low_done = sem("w1_low_done")
        w2_high_done = sem("w2_high_done")
        w2_low_done = sem("w2_low_done")
        h1_summed = sem("h1_summed")
        h1_done = sem("h1_done")
        h1_high_done = sem("h1_high_done")
        h1_low_done = sem("h1_low_done")
        h2_summed = sem("h2_summed")
        h2_done = sem("h2_done")
        y_summed = sem("y_summed")
        y_done = sem("y_done")
        y_stored = sem("y_stored")

        block = ctx.enter_context(nc.Block())

        def selector_at(tile):
            first = QUAD - 1 - 2 * (tile % ZTILES // 4)
            return selector[:, first:first + QUAD]

        @block.sync
        def _(sp):
            def load_raw(k):
                if k >= RAW_SLOTS:
                    sp.wait_ge(w_high_done, k - RAW_SLOTS + 1)
                    sp.wait_ge(w_st_high, 2 * (k - RAW_SLOTS + 1))
                    sp.wait_ge(w_low_done, k - RAW_SLOTS + 1)
                sp.dma_start(raw[:, k % RAW_SLOTS, :], weights[:, k * CHUNK * P:(k + 1) * CHUNK * P]) \
                    .then_inc(raw_loaded[k % RAW_SLOTS], 16)

            def move_low(k):
                sp.wait_ge(w_low_done, k + 1)
                if k >= W_SLOTS:
                    sp.wait_ge(v_done, CHUNK * (k - W_SLOTS + 1))
                sp.dma_start(w_st[EMB:P, k % W_SLOTS, 0, :].bitcast(F32), w_low[0:EMB, k % 2, :].bitcast(F32)) \
                    .then_inc(w_low_moved[k % W_SLOTS], 16)
                sp.dma_start(w_st[0:EMB, k % W_SLOTS, 1, :].bitcast(F32), w_low[EMB:P, k % 2, :].bitcast(F32)) \
                    .then_inc(w_low_moved[k % W_SLOTS], 16)

            def duplicate(m):
                sp.wait_ge(x_copied, 2 * (m + 1))
                sp.wait_ge(x_low_done, m + 1)
                if m >= X_SLOTS:
                    sp.wait_ge(v_done, BLOCK_END[(m - X_SLOTS) | 1])
                for half in range(2):
                    for table in range(2):
                        sp.dma_start(x_dup[half * EMB:(half + 1) * EMB, m % X_SLOTS, table, :, :].bitcast(F32),
                                     x_split[table * EMB:(table + 1) * EMB, m % 2, :, :].bitcast(F32)) \
                            .then_inc(x_dup_moved[m % X_SLOTS], 16)

            sp.dma_start(row_no[:, :], row_no_in).then_inc(row_no_loaded, 16)
            for m in range(LOOKED_UP_BLOCKS):
                sp.dma_start(look_ids[:, m, :, :].rearrange("p a n -> p (a n)"),
                             first_ids[m:m + 1, :].to_broadcast([P, 2 * BATCH])).then_inc(look_loaded[m], 16)
                for table in range(2):
                    sp.dma_start(look_rows[0:LOOKUP_PARTS, m, table, :],
                                 tables[2 * m + table].rearrange("(p k) e -> p (k e)", k=LOOKUP_CHUNKS)) \
                        .then_inc(look_loaded[m], 16)
                if m == 0:
                    load_raw(0)
            for k in range(1, RAW_SLOTS):
                load_raw(k)
            sp.dma_start(ident[:, :], ident_in[:, 0:P + 2 * QUAD]).then_inc(consts_loaded, 16)
            sp.dma_start(selector[:, :], ident_in[:, P + 2 * QUAD:]).then_inc(consts_loaded, 16)
            sp.dma_start(dense_sb[:, :], dense_t).then_inc(consts_loaded, 16)
            for t in range(NSTEPS):
                for k in prep_chunk.get(t, []):
                    if RAW_SLOTS <= k + RAW_SLOTS - 1 < CHUNKS:
                        load_raw(k + RAW_SLOTS - 1)
                    move_low(k)
                for m in prep_block.get(t, []):
                    duplicate(m)
                layer, k = split_mlp_at.get(t + 4, (0, 0))
                if layer:
                    src, dst, loaded, low_done = ((w1, w1_raw, w1_loaded, w1_low_done) if layer == 1 else
                                                  (w2, w2_raw, w2_loaded, w2_low_done))
                    if k >= 1:
                        sp.wait_ge(low_done, k)
                    elif layer == 2:
                        sp.wait_ge(w1_low_done, K1)
                    sp.dma_start(dst[:, :], src[k * P:(k + 1) * P, :]).then_inc(loaded, 16)
                if t == CHUNK:
                    sp.dma_start(b1_sb[:, :], b1).then_inc(mlp_loaded, 16)
                    sp.dma_start(b2_sb[:, :], b2).then_inc(mlp_loaded, 16)
                    sp.dma_start(w3_sb[:, :], w3).then_inc(mlp_loaded, 16)
            sp.wait_ge(y_done, 1)
            sp.dma_start(out, y_sb).then_inc(y_stored, 16)
            sp.wait_ge(y_stored, 16)

        @block.gpsimd
        def _(pool):
            def split_mlp_weights(part):
                layer, k = part
                sb_raw, high, low, high_done, low_done = (
                    (w1_raw, w1_high, w1_low, w1_high_done, w1_low_done) if layer == 1 else
                    (w2_raw, w2_high, w2_low, w2_high_done, w2_low_done))
                pool.wait_ge(high_done, k + 1)
                pool.tensor_tensor(low[:, k, :], sb_raw[:, :], high[:, k, :], ALU.subtract) \
                    .then_inc(low_done, 1)

            pool.dma_start(ids_sb[:, :, :], ids.rearrange("(k p) c -> p k c", p=P)).then_inc(ids_loaded, 16)
            pool.wait_ge(ids_loaded, 16)
            for m in range(LOOKED_UP_BLOCKS, BLOCKS):
                if m - ROW_SLOTS >= LOOKED_UP_BLOCKS:
                    pool.wait_ge(transposed, m - ROW_SLOTS + 1)
                for table in range(2):
                    for k in range(ROWBLKS):
                        c = 2 * m + table
                        pool.indirect_dma_start(
                            rows[:, m % ROW_SLOTS, k, table, :], None, tables[c],
                            bass.IndirectOffsetOnAxis(ap=ids_sb[:, k, c:c + 1], axis=0),
                        ).then_inc(gathered[m], 16)
            for part in mlp_parts:
                split_mlp_weights(part)

        @block.scalar
        def _(act):
            def split_chunk(k):
                act.wait_ge(raw_loaded[k % RAW_SLOTS], 16 * (k // RAW_SLOTS + 1))
                if k >= 2:
                    act.wait_ge(w_low_done, k - 1)
                nc.scalar.activation(w_high[:, k % 2, :], raw[:, k % RAW_SLOTS, :], ACT.Copy) \
                    .then_inc(w_high_done, 1)
                if k >= W_SLOTS:
                    act.wait_ge(v_done, CHUNK * (k - W_SLOTS + 1))
                for tile in range(2):
                    half = slice(tile * EMB, (tile + 1) * EMB)
                    nc.scalar.activation(w_st[half, k % W_SLOTS, tile, :], raw[half, k % RAW_SLOTS, :],
                                         ACT.Copy).then_inc(w_st_high, 1)

            def copy_block(m):
                src = look_ps[:, m, :] if m < LOOKED_UP_BLOCKS else t_ps[:, :]
                act.wait_ge(transposed, m + 1)
                nc.scalar.activation(x_t[:, m, :], src, ACT.Copy).then_inc(x_copied, 1)
                if m >= 2:
                    act.wait_ge(x_dup_moved[(m - 2) % X_SLOTS], 64 * ((m - 2) // X_SLOTS + 1))
                    act.wait_ge(x_low_done, m - 1)
                nc.scalar.activation(x_split[:, m % 2, 0, :], src, ACT.Copy).then_inc(x_copied, 1)

            def z_chunk(n):
                act.wait_ge(reduced, min((n + 1) * ZSTEPS, NSTEPS) // BATCH_STEPS)
                nc.scalar.activation(z_high[:, n, :], z_ps[:, :], ACT.Copy).then_inc(z_high_done, 1)

            for t in range(NSTEPS):
                for k in prep_chunk.get(t, []):
                    split_chunk(k)
                for m in prep_block.get(t, []):
                    copy_block(m)
                if t >= ZSTEPS + 4 and (t - 4) % ZSTEPS == 0:
                    z_chunk((t - 4) // ZSTEPS - 1)
                layer, k = split_mlp_at.get(t, (0, 0))
                if layer == 1:
                    act.wait_ge(w1_loaded, 16 * (k + 1))
                    nc.scalar.activation(w1_high[:, k, :], w1_raw[:, :], ACT.Copy).then_inc(w1_high_done, 1)
                if layer == 2:
                    act.wait_ge(w2_loaded, 16 * (k + 1))
                    nc.scalar.activation(w2_high[:, k, :], w2_raw[:, :], ACT.Copy).then_inc(w2_high_done, 1)
            z_chunk(ZCHUNKS - 1)

            act.wait_ge(mlp_loaded, 48)
            for i in range(K2):
                act.wait_ge(h1_summed, i + 1)
                nc.scalar.activation(h1[:, i, :], h1_ps[:, i, :], ACT.Relu, bias=b1_sb[:, i:i + 1]) \
                    .then_inc(h1_done, 1)
                nc.scalar.activation(h1_high[:, i, :], h1_ps[:, i, :], ACT.Relu, bias=b1_sb[:, i:i + 1]) \
                    .then_inc(h1_high_done, 1)
            for i in range(K3):
                act.wait_ge(h2_summed, i + 1)
                nc.scalar.activation(h2[:, i, :], h2_ps[:, i, :], ACT.Relu, bias=b2_sb[:, i:i + 1]) \
                    .then_inc(h2_done, 1)
            act.wait_ge(y_summed, 1)
            nc.scalar.activation(y_sb, y_ps, ACT.Copy).then_inc(y_done, 1)

        @block.vector
        def _(dve):
            def low_chunk(k):
                dve.wait_ge(w_high_done, k + 1)
                if k >= 2:
                    dve.wait_ge(w_low_moved[(k - 2) % W_SLOTS], 32 * ((k - 2) // W_SLOTS + 1))
                nc.vector.tensor_tensor(w_low[:, k % 2, :], raw[:, k % RAW_SLOTS, :], w_high[:, k % 2, :],
                                        ALU.subtract).then_inc(w_low_done, 1)

            def low_block(m):
                dve.wait_ge(x_copied, 2 * (m + 1))
                if m >= 2:
                    dve.wait_ge(x_dup_moved[(m - 2) % X_SLOTS], 64 * ((m - 2) // X_SLOTS + 1))
                nc.vector.tensor_tensor(x_split[:, m % 2, 1, :], x_t[:, m, :], x_split[:, m % 2, 0, :],
                                        ALU.subtract).then_inc(x_low_done, 1)

            def z_chunk(n):
                dve.wait_ge(z_high_done, n + 1)
                nc.vector.tensor_tensor(z_low[:, n, :], z_ps[:, :], z_high[:, n, :], ALU.subtract) \
                    .then_inc(z_low_done, 1)

            def multiply(t):
                kind, m, j = STEPS[t]
                dve.wait_ge(v_done, t + 1)
                if t >= PROD_SLOTS:
                    dve.wait_ge(reduced, (t - PROD_SLOTS) // BATCH_STEPS + 1)
                if j > m:
                    dve.wait_ge(x_copied, 2 * j + 1)
                if kind == "cross":
                    x = x_t[:, j, :].unsqueeze(1).to_broadcast([P, 2, BATCH])
                else:
                    x = x_t[:, m:m + 2, :]
                nc.vector.tensor_tensor(prod[:, t % PROD_SLOTS, :, :], v_ps[:, t % V_SLOTS, :, :], x,
                                        ALU.mult).then_inc(prod_done, 1)

            def one_hots(m, chunks):
                dve.wait_ge(look_loaded[m], 48)
                for k in chunks:
                    for table in range(2):
                        n = 2 * (m * LOOKUP_CHUNKS + k) + table
                        at = n - 2 * m * LOOKUP_CHUNKS
                        if at >= HOT_SLOTS:
                            dve.wait_ge(one_hot_used, n - HOT_SLOTS + 1 - m)
                        elif m >= 1:
                            dve.wait_ge(transposed, m)
                        nc.vector.tensor_scalar(one_hot[:, n % HOT_SLOTS, :], look_ids[:, m, table, :],
                                                row_no[:, k:k + 1], None, ALU.is_equal) \
                            .then_inc(one_hot_done, 1)

            dve.wait_ge(row_no_loaded, 16)
            one_hots(0, range(LOOKUP_CHUNKS))
            for t in range(NSTEPS):
                for k in prep_chunk.get(t, []):
                    low_chunk(k)
                for m in prep_block.get(t, []):
                    if m + 1 < LOOKED_UP_BLOCKS:
                        one_hots(m + 1, range(LOOKUP_CHUNKS // 2))
                    low_block(m)
                    if m + 1 < LOOKED_UP_BLOCKS:
                        one_hots(m + 1, range(LOOKUP_CHUNKS // 2, LOOKUP_CHUNKS))
                if t >= ZSTEPS + 4 and (t - 4) % ZSTEPS == 0:
                    z_chunk((t - 4) // ZSTEPS - 1)
                multiply(t)
            z_chunk(ZCHUNKS - 1)
            for i in range(K2):
                dve.wait_ge(h1_done, i + 1)
                dve.wait_ge(h1_high_done, i + 1)
                nc.vector.tensor_tensor(h1_low[:, i, :], h1[:, i, :], h1_high[:, i, :], ALU.subtract) \
                    .then_inc(h1_low_done, 1)

        @block.tensor
        def _(pe):
            def look_up_block(m):
                pe.wait_ge(look_loaded[m], 48)
                for k in range(LOOKUP_CHUNKS):
                    for table in range(2):
                        n = 2 * (m * LOOKUP_CHUNKS + k) + table
                        pe.wait_ge(one_hot_done, n + 1)
                        last = nc.tensor.matmul(
                            look_ps[table * EMB:(table + 1) * EMB, m, :],
                            look_rows[0:LOOKUP_PARTS, m, table, k * EMB:(k + 1) * EMB],
                            one_hot[0:LOOKUP_PARTS, n % HOT_SLOTS, :],
                            start=(k == 0), stop=(k == LOOKUP_CHUNKS - 1))
                        if k < LOOKUP_CHUNKS - 1 or table == 0:
                            last.then_inc(one_hot_used, 1)
                last.then_inc(transposed, 1)

            def transpose_block(m):
                if m == LOOKED_UP_BLOCKS:
                    pe.wait_ge(consts_loaded, 48)
                pe.wait_ge(gathered[m], 16 * 2 * ROWBLKS)
                if m > LOOKED_UP_BLOCKS:
                    pe.wait_ge(x_copied, 2 * m)
                for k in range(ROWBLKS):
                    last = nc.tensor.transpose(
                        t_ps[:, k * P:(k + 1) * P],
                        rows[:, m % ROW_SLOTS, k, :, :].rearrange("p c e -> p (c e)"),
                        ident[:, QUAD:QUAD + P])
                last.then_inc(transposed, 1)

            def bilinear(t):
                kind, m, j = STEPS[t]
                k, at = divmod(t, CHUNK)
                if at == 0:
                    pe.wait_ge(w_st_high, 2 * (k + 1))
                    pe.wait_ge(w_low_moved[k % W_SLOTS], 32 * (k // W_SLOTS + 1))
                newest = m if kind == "cross" else j
                pe.wait_ge(x_dup_moved[newest % X_SLOTS], 64 * (newest // X_SLOTS + 1))
                if t >= V_SLOTS:
                    pe.wait_ge(prod_done, t - V_SLOTS + 1)
                elif t == V_SLOTS - 1:
                    pe.wait_ge(x_copied, 2 * LOOKED_UP_BLOCKS)
                for tile in range(2):
                    blk, table = (m, tile) if kind == "cross" else ((m, j)[tile], 1)
                    for part in range(2):
                        last = nc.tensor.matmul(
                            v_ps[:, t % V_SLOTS, tile, :],
                            w_st[:, k % W_SLOTS, tile, at * P:(at + 1) * P],
                            x_dup[:, blk % X_SLOTS, table, part, :],
                            start=(part == 0), stop=(part == 1))
                last.then_inc(v_done, 1)

            def reduce_batch(n):
                t0 = n * BATCH_STEPS
                chunk = t0 // ZSTEPS
                pe.wait_ge(prod_done, t0 + BATCH_STEPS)
                if t0 % ZSTEPS == 0 and chunk >= 1:
                    pe.wait_ge(z_high_done, chunk)
                    pe.wait_ge(z_low_done, chunk)
                tiles = min(ZTILES, 2 * NSTEPS - chunk * ZTILES)
                for i in range(2 * BATCH_STEPS):
                    step, tile = t0 + i // 2, 2 * t0 + i
                    quad = tile % 4
                    at = tile % ZTILES
                    dense_follows = quad == 0 and chunk == ZCHUNKS - 1
                    last = nc.tensor.matmul(z_ps[quad * QUAD:(quad + 1) * QUAD, :], selector_at(tile),
                                            prod[:, step % PROD_SLOTS, i % 2, :],
                                            start=(at < 4), stop=(at >= tiles - 4 and not dense_follows))
                if t0 == NSTEPS - BATCH_STEPS:
                    last = nc.tensor.matmul(z_ps[0:QUAD, :],
                                            ident[0:DENSE, QUAD - DENSE_ROW:2 * QUAD - DENSE_ROW],
                                            dense_sb[:, :], start=False, stop=True)
                last.then_inc(reduced, 1)

            for t in range(NSTEPS):
                for m in prep_block.get(t, []):
                    if m < LOOKED_UP_BLOCKS:
                        look_up_block(m)
                    else:
                        transpose_block(m)
                bilinear(t)
                if t >= V_SLOTS and (t - V_SLOTS) % BATCH_STEPS == BATCH_STEPS - 1:
                    reduce_batch((t - V_SLOTS) // BATCH_STEPS)
            for n in range((NSTEPS - 1 - V_SLOTS - BATCH_STEPS + 1) // BATCH_STEPS + 1, NSTEPS // BATCH_STEPS):
                reduce_batch(n)

            def layer(out_ps, w_hi, w_lo, in_hi, in_lo, chunks, in_ready, summed):
                for n in range(chunks):
                    if in_ready is not None:
                        in_ready(n)
                    for p, (w, x) in enumerate(((w_hi, in_hi), (w_lo, in_hi), (w_hi, in_lo))):
                        last = nc.tensor.matmul(out_ps, w(n), x(n), start=(n == 0 and p == 0),
                                                stop=(n == chunks - 1 and p == 2))
                last.then_inc(summed, 1)

            pe.wait_ge(prod_done, NSTEPS)
            pe.wait_ge(w1_high_done, K1)
            pe.wait_ge(w1_low_done, K1)

            def z_ready(n):
                pe.wait_ge(z_high_done, n + 1)
                pe.wait_ge(z_low_done, n + 1)

            def h1_ready(n):
                pe.wait_ge(h1_high_done, n + 1)
                pe.wait_ge(h1_low_done, n + 1)

            for i in range(K2):
                cols = slice(i * P, (i + 1) * P)
                layer(h1_ps[:, i, :], lambda n: w1_high[:, n, cols], lambda n: w1_low[:, n, cols],
                      lambda n: z_high[:, n, :], lambda n: z_low[:, n, :], K1, z_ready if i == 0 else None,
                      h1_summed)
            pe.wait_ge(w2_high_done, K2)
            pe.wait_ge(w2_low_done, K2)
            for i in range(K3):
                cols = slice(i * P, (i + 1) * P)
                layer(h2_ps[:, i, :], lambda n: w2_high[:, n, cols], lambda n: w2_low[:, n, cols],
                      lambda n: h1_high[:, n, :], lambda n: h1_low[:, n, :], K2, h1_ready if i == 0 else None,
                      h2_summed)
            pe.wait_ge(mlp_loaded, 48)
            pe.wait_ge(x_copied, 2 * BLOCKS)
            for n in range(K3):
                pe.wait_ge(h2_done, n + 1)
                last = nc.tensor.matmul(y_ps, w3_sb[:, n:n + 1], h2[:, n, :], start=(n == 0),
                                        stop=(n == K3 - 1))
            last.then_inc(y_summed, 1)


def kernel(**inputs):
    import numpy as np
    import concourse.bacc as bacc
    from concourse.bass_utils import run_bass_kernel_spmd

    pair_of = {}
    for r in range(TABLES - 1):
        for c in range(r + 1, TABLES):
            pair_of[(r, c)] = len(pair_of)
    tiles = tile_pairs()

    table_at = table_order([inputs[f"tbl_{c}"].shape[0] for c in range(TABLES)])
    places = {a: i for i, a in enumerate(table_at)}
    assert sorted(places) == list(range(TABLES))

    def pair(rc):
        a, b = table_at[rc[0]], table_at[rc[1]]
        return pair_of[(min(a, b), max(a, b))], a > b

    param = np.asarray(inputs["L0_rec_param"]).transpose(1, 0, 2)
    npairs = param.shape[0]
    both_ways = np.concatenate([param, param.transpose(0, 2, 1), np.zeros((1, EMB, EMB), param.dtype)])
    order = np.array([[2 * npairs if rc is None else pair(rc)[0] + npairs * pair(rc)[1] for rc in t]
                      for t in tiles])
    weights = both_ways[order.reshape(NSTEPS, 2, 2)]
    weights = np.ascontiguousarray(weights.transpose(1, 3, 0, 2, 4).reshape(P, NSTEPS * P))

    w_top1 = np.asarray(inputs["W_top1"])
    w1 = np.zeros((ZCHUNKS * P, HID1), w_top1.dtype)
    for t, pairs in enumerate(tiles):
        for odd, rc in enumerate(pairs):
            if rc is not None:
                w1[z_row(t, odd)] = w_top1[pair(rc)[0]]
    dense_at = (ZCHUNKS - 1) * P + DENSE_ROW
    w1[dense_at:dense_at + DENSE] = w_top1[npairs:]

    consts = np.zeros((P, P + 4 * QUAD), np.float32)
    consts[:, QUAD:QUAD + P] = np.eye(P, dtype=np.float32)
    consts[0:EMB, P + 2 * QUAD + QUAD - 1] = 1.0
    consts[EMB:P, P + 2 * QUAD + QUAD] = 1.0

    arrays = {
        "dense_t": np.ascontiguousarray(np.asarray(inputs["dense_ctx"]).T),
        "ids": np.ascontiguousarray(np.asarray(inputs["ids"])[:, table_at]),
        "first_ids": np.ascontiguousarray(
            np.asarray(inputs["ids"]).T[table_at[:2 * LOOKED_UP_BLOCKS]].reshape(LOOKED_UP_BLOCKS, -1)),
        "weights": weights,
        "w1": w1,
        "b1": np.ascontiguousarray(np.asarray(inputs["b_top1"]).reshape(-1, P).T),
        "w2": np.ascontiguousarray(inputs["W_top2"]),
        "b2": np.ascontiguousarray(np.asarray(inputs["b_top2"]).reshape(-1, P).T),
        "w3": np.ascontiguousarray(np.asarray(inputs["W_top3"]).reshape(-1, P).T),
        "consts": consts,
        "row_numbers": np.arange(P * LOOKUP_CHUNKS, dtype=np.float32).reshape(P, LOOKUP_CHUNKS),
    }
    for c in range(TABLES):
        arrays[f"tbl_{c}"] = np.ascontiguousarray(inputs[f"tbl_{c}"])

    nc = bacc.Bacc("TRN2", target_bir_lowering=False, num_devices=1)
    dram = {name: nc.dram_tensor(name, a.shape, mybir.dt.from_np(a.dtype), kind="ExternalInput").ap()
            for name, a in arrays.items()}
    y = nc.dram_tensor("y", (1, BATCH), F32, kind="ExternalOutput").ap()
    dlrm_tower(nc, dram["dense_t"], dram["ids"], dram["first_ids"], [dram[f"tbl_{c}"] for c in table_at],
               dram["weights"],
               dram["w1"], dram["b1"], dram["w2"], dram["b2"], dram["w3"], dram["consts"], dram["row_numbers"], y)
    result = run_bass_kernel_spmd(nc, [arrays], core_ids=[0])
    return result.results[0]["y"].reshape(BATCH, 1)
```

```python
from contextlib import ExitStack

import concourse.bass as bass
from concourse import mybir

P = 128
BATCH = 512
TABLES = 40
EMB = 64
DENSE = 16
HID1 = 512
HID2 = 256

BLOCKS = TABLES // 2
ROWBLKS = BATCH // P
QUAD = 32

F32 = mybir.dt.float32
F32R = mybir.dt.float32r
I32 = mybir.dt.int32
ALU = mybir.AluOpType
ACT = mybir.ActivationFunctionType


def plan_steps():
    steps, ends = [], []
    for m in range(BLOCKS):
        steps += [("cross", m, j) for j in range(m)] if m > 1 else [("cross", 0, 1)] * m
        if m % 2:
            steps.append(("diag", m - 1, m))
        ends.append(len(steps))
    return steps, ends


def tile_pairs():
    tiles = []
    for kind, m, j in plan_steps()[0]:
        if kind == "cross":
            tiles += [((2 * j, c), (2 * j + 1, c)) for c in (2 * m, 2 * m + 1)]
        else:
            tiles += [((2 * k, 2 * k + 1), None) for k in (m, j)]
    return tiles


def table_order(rows_of):
    first = [c for c, n in enumerate(rows_of) if n == LOOKUP_ROWS][:2 * len(LOOKED_UP)]
    assert len(first) == 2 * len(LOOKED_UP)
    others = [c for c in range(len(rows_of)) if c not in first]
    return [(first if place // 2 in LOOKED_UP else others).pop(0) for place in range(len(rows_of))]


STEPS, BLOCK_END = plan_steps()
NSTEPS = len(STEPS)
CHUNK = 4
CHUNKS = NSTEPS // CHUNK
BATCH_STEPS = 4
ZTILES = P // QUAD * (QUAD // 2)
ZSTEPS = ZTILES // 2
ZCHUNKS = -(-NSTEPS // ZSTEPS)
DENSE_ROW = 8


def z_row(tile, odd):
    chunk, at = divmod(tile, ZTILES)
    return chunk * P + (at % 4) * QUAD + 2 * (at // 4) + odd


RAW_SLOTS = 3
W_SLOTS = 3
X_SLOTS = 3
V_SLOTS = 3
PROD_SLOTS = 8
LOOKED_UP = (0, 3)
LOOKUP_ROWS = 1000
LOOKUP_CHUNKS = 8
LOOKUP_PARTS = LOOKUP_ROWS // LOOKUP_CHUNKS
HOT_SLOTS = 4
POOL_CHUNKS = 30
BLOCK_LEAD = 10
RAMP_LEAD = 6
RAMP_BLOCKS = 9
ROW_SLOTS = 4


def block_prep_at():
    at = {0: [0, 1], 1: [2], 2: [3], 3: [4]}
    for m in range(5, BLOCKS):
        lead = RAMP_LEAD if m < RAMP_BLOCKS else BLOCK_LEAD
        at.setdefault(max(BLOCK_END[m - 2], BLOCK_END[m - 1] - lead), []).append(m)
    return at


def chunk_prep_at():
    at = {0: [0], 1: [1], 3: [2]}
    for k in range(3, CHUNKS):
        at.setdefault(CHUNK * (k - 2) + 1, []).append(k)
    return at


def dlrm_tower(nc, dense_t, ids, first_ids, tables, weights, w1, b1, w2, b2, w3, ident_in, row_no_in, out):
    assert NSTEPS % CHUNK == 0 and NSTEPS % BATCH_STEPS == 0
    prep_block, prep_chunk = block_prep_at(), chunk_prep_at()
    K1 = ZCHUNKS
    K2 = HID1 // P
    K3 = HID2 // P
    mlp_parts = [(1, k) for k in range(K1)] + [(2, k) for k in range(K2)]
    split_mlp_at = {2 * NSTEPS // 3 + 5 * i: part for i, part in enumerate(mlp_parts)}

    with ExitStack() as ctx:
        def sb(name, shape, dt):
            return ctx.enter_context(nc.sbuf_tensor(name, shape, dt))

        def sem(name):
            return ctx.enter_context(nc.semaphore(name))

        ident = sb("ident", [P, P + 2 * QUAD], F32)
        selector = sb("selector", [P, 2 * QUAD], F32)
        ids_sb = sb("ids_sb", [P, ROWBLKS, TABLES], I32)
        rows = sb("rows", [P, ROW_SLOTS, ROWBLKS, 2, EMB], F32)
        x_t = sb("x_t", [P, BLOCKS, BATCH], F32)
        x_split = sb("x_split", [P, 2, 2, BATCH], F32R)
        x_dup = sb("x_dup", [P, X_SLOTS, 2, 2, BATCH], F32R)
        raw = sb("raw", [P, RAW_SLOTS, CHUNK * P], F32)
        w_high = sb("w_high", [P, 2, CHUNK * P], F32R)
        w_low = sb("w_low", [P, 2, CHUNK * P], F32R)
        w_st = sb("w_st", [P, W_SLOTS, 2, CHUNK * P], F32R)
        prod = sb("prod", [P, PROD_SLOTS, 2, BATCH], F32)
        z_high = sb("z_high", [P, K1, BATCH], F32R)
        z_low = sb("z_low", [P, K1, BATCH], F32R)
        w3_sb = sb("w3_sb", [P, K3], F32)
        b1_sb = sb("b1_sb", [P, K2], F32)
        b2_sb = sb("b2_sb", [P, K3], F32)
        dense_sb = sb("dense_sb", [DENSE, BATCH], F32)
        row_no = sb("row_no", [P, LOOKUP_CHUNKS], F32)
        w1_raw = sb("w1_raw", [P, HID1], F32)
        w1_high = sb("w1_high", [P, K1, HID1], F32R)
        w1_low = sb("w1_low", [P, K1, HID1], F32R)
        w2_raw = w1_raw[:, 0:HID2]
        w2_high = sb("w2_high", [P, K2, HID2], F32R)
        w2_low = sb("w2_low", [P, K2, HID2], F32R)
        look_ids = prod[:, 0:PROD_SLOTS:4, :, :].bitcast(I32)
        look_rows = prod[:, 1:PROD_SLOTS:4, :, :]
        one_hot = prod[:, PROD_SLOTS - HOT_SLOTS // 2:, :, :].rearrange("p a b n -> p (a b) n")
        assert BLOCK_END[LOOKED_UP[1] - 1] <= 4 and PROD_SLOTS == 8 and LOOKUP_CHUNKS * EMB == BATCH
        h1 = prod[:, 0:2, :, :].rearrange("p a b n -> p (a b) n")
        h1_high = x_dup[:, 0, :, :, :].rearrange("p a b n -> p (a b) n")
        h1_low = x_dup[:, 1, :, :, :].rearrange("p a b n -> p (a b) n")
        h2 = prod[:, 4, :, :]
        y_sb = prod[:, 5, 0, 0:ROWBLKS]

        v_ps = ctx.enter_context(nc.psum_tensor("v_ps", [P, V_SLOTS, 2, BATCH], F32))
        z_ps = ctx.enter_context(nc.psum_tensor("z_ps", [P, BATCH], F32))
        t_ps = ctx.enter_context(nc.psum_tensor("t_ps", [P, BATCH], F32))
        third_last, second_last, last_slot = [(NSTEPS - i) % V_SLOTS for i in (3, 2, 1)]
        h1_ps = [v_ps[:, slot, half, :] for slot in (third_last, second_last) for half in range(2)]
        h2_ps = v_ps[:, last_slot, :, :]
        y_ps = t_ps[:, 0:ROWBLKS]
        look_ps = (v_ps[:, V_SLOTS - 1, 0, :], z_ps[:, :])

        consts_loaded = sem("consts_loaded")
        ids_loaded = sem("ids_loaded")
        row_no_loaded = sem("row_no_loaded")
        mlp_loaded = sem("mlp_loaded")
        w1_loaded = sem("w1_loaded")
        w2_loaded = sem("w2_loaded")
        look_loaded = [sem(f"look_loaded{m}") for m in LOOKED_UP]
        one_hot_done = sem("one_hot_done")
        one_hot_used = sem("one_hot_used")
        gathered = [sem(f"gathered{m}") for m in range(BLOCKS)]
        transposed = sem("transposed")
        x_high_done = sem("x_high_done")
        x_copied = sem("x_copied")
        x_low_done = sem("x_low_done")
        x_own_done = sem("x_own_done")
        x_dup_moved = [sem(f"x_dup_moved{i}") for i in range(X_SLOTS)]
        raw_loaded = [sem(f"raw_loaded{i}") for i in range(RAW_SLOTS)]
        w_high_done = sem("w_high_done")
        w_st_high = sem("w_st_high")
        w_low_done = sem("w_low_done")
        w_low_by_pool = sem("w_low_by_pool")
        w_low_moved = [sem(f"w_low_moved{i}") for i in range(W_SLOTS)]
        v_done = sem("v_done")
        prod_done = sem("prod_done")
        reduced = sem("reduced")
        z_high_done = sem("z_high_done")
        z_low_done = sem("z_low_done")
        w1_high_done = sem("w1_high_done")
        w1_low_done = sem("w1_low_done")
        w2_high_done = sem("w2_high_done")
        w2_low_done = sem("w2_low_done")
        h1_summed = sem("h1_summed")
        h1_done = sem("h1_done")
        h1_high_done = sem("h1_high_done")
        h1_low_done = sem("h1_low_done")
        h2_summed = sem("h2_summed")
        h2_done = sem("h2_done")
        y_summed = sem("y_summed")
        y_done = sem("y_done")
        y_stored = sem("y_stored")

        block = ctx.enter_context(nc.Block())

        def selector_at(tile):
            first = QUAD - 1 - 2 * (tile % ZTILES // 4)
            return selector[:, first:first + QUAD]

        def wait_low(engine, k):
            if k < POOL_CHUNKS:
                engine.wait_ge(w_low_done, k + 1)
            else:
                engine.wait_ge(w_low_by_pool, k - POOL_CHUNKS + 1)

        @block.sync
        def _(sp):
            def load_raw(k):
                if k >= RAW_SLOTS:
                    sp.wait_ge(w_high_done, k - RAW_SLOTS + 1)
                    sp.wait_ge(w_st_high, 2 * (k - RAW_SLOTS + 1))
                    wait_low(sp, k - RAW_SLOTS)
                sp.dma_start(raw[:, k % RAW_SLOTS, :], weights[:, k * CHUNK * P:(k + 1) * CHUNK * P]) \
                    .then_inc(raw_loaded[k % RAW_SLOTS], 16)

            def move_low(k):
                wait_low(sp, k)
                if k >= W_SLOTS:
                    sp.wait_ge(v_done, CHUNK * (k - W_SLOTS + 1))
                sp.dma_start(w_st[EMB:P, k % W_SLOTS, 0, :].bitcast(F32), w_low[0:EMB, k % 2, :].bitcast(F32)) \
                    .then_inc(w_low_moved[k % W_SLOTS], 16)
                sp.dma_start(w_st[0:EMB, k % W_SLOTS, 1, :].bitcast(F32), w_low[EMB:P, k % 2, :].bitcast(F32)) \
                    .then_inc(w_low_moved[k % W_SLOTS], 16)

            def duplicate(m):
                sp.wait_ge(x_high_done, m + 1)
                sp.wait_ge(x_low_done, m + 1)
                if m >= X_SLOTS:
                    sp.wait_ge(v_done, BLOCK_END[(m - X_SLOTS) | 1])
                for table in (1, 0):
                    other = slice((1 - table) * EMB, (2 - table) * EMB)
                    sp.dma_start(x_dup[other, m % X_SLOTS, table, :, :].bitcast(F32),
                                 x_split[table * EMB:(table + 1) * EMB, m % 2, :, :].bitcast(F32)) \
                        .then_inc(x_dup_moved[m % X_SLOTS], 16)

            def load_look_up(i):
                for table in range(2):
                    sp.dma_start(look_ids[:, i, table, :],
                                 first_ids[2 * i + table:2 * i + table + 1, :].to_broadcast([P, BATCH])) \
                        .then_inc(look_loaded[i], 16)
                    sp.dma_start(look_rows[0:LOOKUP_PARTS, i, table, :],
                                 tables[2 * LOOKED_UP[i] + table].rearrange("(p k) e -> p (k e)", k=LOOKUP_CHUNKS)) \
                        .then_inc(look_loaded[i], 16)

            sp.dma_start(row_no[:, :], row_no_in).then_inc(row_no_loaded, 16)
            load_look_up(0)
            load_raw(0)
            sp.dma_start(ident[:, :], ident_in[:, 0:P + 2 * QUAD]).then_inc(consts_loaded, 16)
            load_look_up(1)
            for k in range(1, RAW_SLOTS):
                load_raw(k)
            sp.dma_start(selector[:, :], ident_in[:, P + 2 * QUAD:]).then_inc(consts_loaded, 16)
            sp.dma_start(dense_sb[:, :], dense_t).then_inc(consts_loaded, 16)
            move_low(0)
            for t in range(NSTEPS):
                for m in prep_block.get(t, []):
                    duplicate(m)
                for k in prep_chunk.get(t, []):
                    if RAW_SLOTS <= k + RAW_SLOTS - 1 < CHUNKS:
                        load_raw(k + RAW_SLOTS - 1)
                    if k > 0:
                        move_low(k)
                layer, k = split_mlp_at.get(t + 4, (0, 0))
                if layer:
                    src, dst, loaded, low_done = ((w1, w1_raw, w1_loaded, w1_low_done) if layer == 1 else
                                                  (w2, w2_raw, w2_loaded, w2_low_done))
                    if k >= 1:
                        sp.wait_ge(low_done, k)
                    elif layer == 2:
                        sp.wait_ge(w1_low_done, K1)
                    sp.dma_start(dst[:, :], src[k * P:(k + 1) * P, :]).then_inc(loaded, 16)
                if t == CHUNK:
                    sp.dma_start(b1_sb[:, :], b1).then_inc(mlp_loaded, 16)
                    sp.dma_start(b2_sb[:, :], b2).then_inc(mlp_loaded, 16)
                    sp.dma_start(w3_sb[:, :], w3).then_inc(mlp_loaded, 16)
            sp.wait_ge(y_done, 1)
            sp.dma_start(out, y_sb).then_inc(y_stored, 16)
            sp.wait_ge(y_stored, 16)

        @block.gpsimd
        def _(pool):
            def split_mlp_weights(part):
                layer, k = part
                sb_raw, high, low, high_done, low_done = (
                    (w1_raw, w1_high, w1_low, w1_high_done, w1_low_done) if layer == 1 else
                    (w2_raw, w2_high, w2_low, w2_high_done, w2_low_done))
                pool.wait_ge(high_done, k + 1)
                pool.tensor_tensor(low[:, k, :], sb_raw[:, :], high[:, k, :], ALU.subtract) \
                    .then_inc(low_done, 1)

            def low_chunk(k):
                pool.wait_ge(w_high_done, k + 1)
                pool.wait_ge(w_low_moved[(k - 2) % W_SLOTS], 32 * ((k - 2) // W_SLOTS + 1))
                pool.tensor_tensor(w_low[:, k % 2, :], raw[:, k % RAW_SLOTS, :], w_high[:, k % 2, :],
                                   ALU.subtract).then_inc(w_low_by_pool, 1)

            pool.dma_start(ids_sb[:, :, :], ids.rearrange("(k p) c -> p k c", p=P)).then_inc(ids_loaded, 16)
            pool.wait_ge(ids_loaded, 16)
            for m in range(BLOCKS):
                if m in LOOKED_UP:
                    continue
                if m >= ROW_SLOTS:
                    pool.wait_ge(transposed, m - ROW_SLOTS + 1)
                for table in range(2):
                    for k in range(ROWBLKS):
                        c = 2 * m + table
                        pool.indirect_dma_start(
                            rows[:, m % ROW_SLOTS, k, table, :], None, tables[c],
                            bass.IndirectOffsetOnAxis(ap=ids_sb[:, k, c:c + 1], axis=0),
                        ).then_inc(gathered[m], 16)
            for t in range(NSTEPS):
                for k in prep_chunk.get(t, []):
                    if k >= POOL_CHUNKS:
                        low_chunk(k)
                if t in split_mlp_at:
                    split_mlp_weights(split_mlp_at[t])

        @block.scalar
        def _(act):
            def split_chunk(k):
                act.wait_ge(raw_loaded[k % RAW_SLOTS], 16 * (k // RAW_SLOTS + 1))
                if k >= 2:
                    wait_low(act, k - 2)
                nc.scalar.activation(w_high[:, k % 2, :], raw[:, k % RAW_SLOTS, :], ACT.Copy) \
                    .then_inc(w_high_done, 1)
                if k >= W_SLOTS:
                    act.wait_ge(v_done, CHUNK * (k - W_SLOTS + 1))
                for tile in range(2):
                    half = slice(tile * EMB, (tile + 1) * EMB)
                    nc.scalar.activation(w_st[half, k % W_SLOTS, tile, :], raw[half, k % RAW_SLOTS, :],
                                         ACT.Copy).then_inc(w_st_high, 1)

            def split_block(m):
                src = look_ps[LOOKED_UP.index(m)] if m in LOOKED_UP else t_ps[:, :]
                act.wait_ge(transposed, m + 1)
                if m >= 2:
                    act.wait_ge(x_dup_moved[(m - 2) % X_SLOTS], 32 * ((m - 2) // X_SLOTS + 1))
                    act.wait_ge(x_low_done, m - 1)
                nc.scalar.activation(x_split[:, m % 2, 0, :], src, ACT.Copy).then_inc(x_high_done, 1)
                nc.scalar.activation(x_t[:, m, :], src, ACT.Copy).then_inc(x_copied, 1)
                if m >= X_SLOTS:
                    act.wait_ge(v_done, BLOCK_END[(m - X_SLOTS) | 1])
                for part in range(2):
                    if part == 1:
                        act.wait_ge(x_low_done, m + 1)
                    for table in (1, 0):
                        half = slice(table * EMB, (table + 1) * EMB)
                        part_src = x_split[half, m % 2, 1, :] if part else src[half, :]
                        nc.scalar.activation(x_dup[half, m % X_SLOTS, table, part, :], part_src, ACT.Copy) \
                            .then_inc(x_own_done, 1)

            def z_chunk(n):
                act.wait_ge(reduced, min((n + 1) * ZSTEPS, NSTEPS) // BATCH_STEPS)
                nc.scalar.activation(z_high[:, n, :], z_ps[:, :], ACT.Copy).then_inc(z_high_done, 1)

            split_chunk(0)
            for t in range(NSTEPS):
                for m in prep_block.get(t, []):
                    split_block(m)
                for k in prep_chunk.get(t, []):
                    if k > 0:
                        split_chunk(k)
                if t >= ZSTEPS + 4 and (t - 4) % ZSTEPS == 0:
                    z_chunk((t - 4) // ZSTEPS - 1)
                layer, k = split_mlp_at.get(t, (0, 0))
                if layer == 1:
                    act.wait_ge(w1_loaded, 16 * (k + 1))
                    nc.scalar.activation(w1_high[:, k, :], w1_raw[:, :], ACT.Copy).then_inc(w1_high_done, 1)
                if layer == 2:
                    act.wait_ge(w2_loaded, 16 * (k + 1))
                    nc.scalar.activation(w2_high[:, k, :], w2_raw[:, :], ACT.Copy).then_inc(w2_high_done, 1)
            z_chunk(ZCHUNKS - 1)

            act.wait_ge(mlp_loaded, 48)
            for i in range(K2):
                act.wait_ge(h1_summed, i + 1)
                nc.scalar.activation(h1[:, i, :], h1_ps[i], ACT.Relu, bias=b1_sb[:, i:i + 1]) \
                    .then_inc(h1_done, 1)
                nc.scalar.activation(h1_high[:, i, :], h1_ps[i], ACT.Relu, bias=b1_sb[:, i:i + 1]) \
                    .then_inc(h1_high_done, 1)
            for i in range(K3):
                act.wait_ge(h2_summed, i + 1)
                nc.scalar.activation(h2[:, i, :], h2_ps[:, i, :], ACT.Relu, bias=b2_sb[:, i:i + 1]) \
                    .then_inc(h2_done, 1)
            act.wait_ge(y_summed, 1)
            nc.scalar.activation(y_sb, y_ps, ACT.Copy).then_inc(y_done, 1)

        @block.vector
        def _(dve):
            def low_chunk(k):
                dve.wait_ge(w_high_done, k + 1)
                if k >= 2:
                    dve.wait_ge(w_low_moved[(k - 2) % W_SLOTS], 32 * ((k - 2) // W_SLOTS + 1))
                nc.vector.tensor_tensor(w_low[:, k % 2, :], raw[:, k % RAW_SLOTS, :], w_high[:, k % 2, :],
                                        ALU.subtract).then_inc(w_low_done, 1)

            def low_block(m):
                dve.wait_ge(x_high_done, m + 1)
                dve.wait_ge(x_copied, m + 1)
                if m >= 2:
                    dve.wait_ge(x_dup_moved[(m - 2) % X_SLOTS], 32 * ((m - 2) // X_SLOTS + 1))
                    dve.wait_ge(x_own_done, 4 * (m - 1))
                nc.vector.tensor_tensor(x_split[:, m % 2, 1, :], x_t[:, m, :], x_split[:, m % 2, 0, :],
                                        ALU.subtract).then_inc(x_low_done, 1)

            def z_chunk(n):
                dve.wait_ge(z_high_done, n + 1)
                nc.vector.tensor_tensor(z_low[:, n, :], z_ps[:, :], z_high[:, n, :], ALU.subtract) \
                    .then_inc(z_low_done, 1)

            def multiply(t):
                kind, m, j = STEPS[t]
                dve.wait_ge(v_done, t + 1)
                if t >= PROD_SLOTS:
                    dve.wait_ge(reduced, (t - PROD_SLOTS) // BATCH_STEPS + 1)
                if j > m:
                    dve.wait_ge(x_copied, j + 1)
                if kind == "cross":
                    x = x_t[:, j, :].unsqueeze(1).to_broadcast([P, 2, BATCH])
                else:
                    x = x_t[:, m:m + 2, :]
                nc.vector.tensor_tensor(prod[:, t % PROD_SLOTS, :, :], v_ps[:, t % V_SLOTS, :, :], x,
                                        ALU.mult).then_inc(prod_done, 1)

            def one_hots(i, chunks):
                dve.wait_ge(look_loaded[i], 64)
                for k in chunks:
                    for table in range(2):
                        at = 2 * k + table
                        n = 2 * i * LOOKUP_CHUNKS + at
                        if at >= HOT_SLOTS:
                            dve.wait_ge(one_hot_used, n - HOT_SLOTS + 1 - i)
                        elif i >= 1:
                            dve.wait_ge(transposed, LOOKED_UP[i - 1] + 1)
                        nc.vector.tensor_scalar(one_hot[:, n % HOT_SLOTS, :], look_ids[:, i, table, :],
                                                row_no[:, k:k + 1], None, ALU.is_equal) \
                            .then_inc(one_hot_done, 1)

            dve.wait_ge(row_no_loaded, 16)
            one_hots(0, range(5))
            low_chunk(0)
            one_hots(0, range(5, LOOKUP_CHUNKS))
            one_hots(1, range(1))
            for t in range(NSTEPS):
                for m in prep_block.get(t, []):
                    if m == 1:
                        one_hots(1, range(1, 3))
                    low_block(m)
                if t >= ZSTEPS + 4 and (t - 4) % ZSTEPS == 0:
                    z_chunk((t - 4) // ZSTEPS - 1)
                if t == 0:
                    one_hots(1, range(3, 6))
                if t == 1:
                    one_hots(1, range(6, LOOKUP_CHUNKS))
                multiply(t)
                for k in prep_chunk.get(t, []):
                    if 0 < k < POOL_CHUNKS:
                        low_chunk(k)
            z_chunk(ZCHUNKS - 1)
            for i in range(K2):
                dve.wait_ge(h1_done, i + 1)
                dve.wait_ge(h1_high_done, i + 1)
                nc.vector.tensor_tensor(h1_low[:, i, :], h1[:, i, :], h1_high[:, i, :], ALU.subtract) \
                    .then_inc(h1_low_done, 1)

        @block.tensor
        def _(pe):
            def look_up_block(i, chunks):
                pe.wait_ge(look_loaded[i], 64)
                for k in chunks:
                    for table in range(2):
                        n = 2 * (i * LOOKUP_CHUNKS + k) + table
                        pe.wait_ge(one_hot_done, n + 1)
                        last = nc.tensor.matmul(
                            look_ps[i][table * EMB:(table + 1) * EMB, :],
                            look_rows[0:LOOKUP_PARTS, i, table, k * EMB:(k + 1) * EMB],
                            one_hot[0:LOOKUP_PARTS, n % HOT_SLOTS, :],
                            start=(k == 0), stop=(k == LOOKUP_CHUNKS - 1))
                        done = k == LOOKUP_CHUNKS - 1 and table == 1
                        last.then_inc(transposed if done else one_hot_used, 1)

            def transpose_block(m):
                if m == 1:
                    pe.wait_ge(consts_loaded, 48)
                pe.wait_ge(gathered[m], 16 * 2 * ROWBLKS)
                if m > 1:
                    before = m - 2 if m - 1 in LOOKED_UP else m - 1
                    pe.wait_ge(x_own_done, 4 * before + 2)
                for k in range(ROWBLKS):
                    last = nc.tensor.transpose(
                        t_ps[:, k * P:(k + 1) * P],
                        rows[:, m % ROW_SLOTS, k, :, :].rearrange("p c e -> p (c e)"),
                        ident[:, QUAD:QUAD + P])
                last.then_inc(transposed, 1)

            def bilinear(t):
                kind, m, j = STEPS[t]
                k, at = divmod(t, CHUNK)
                if at == 0:
                    pe.wait_ge(w_st_high, 2 * (k + 1))
                    pe.wait_ge(w_low_moved[k % W_SLOTS], 32 * (k // W_SLOTS + 1))
                newest = m if kind == "cross" else j
                pe.wait_ge(x_own_done, 4 * (newest + 1))
                pe.wait_ge(x_dup_moved[newest % X_SLOTS], 32 * (newest // X_SLOTS + 1))
                if t >= V_SLOTS:
                    pe.wait_ge(prod_done, t - V_SLOTS + 1)
                for tile in range(2):
                    blk, table = (m, tile) if kind == "cross" else ((m, j)[tile], 1)
                    for part in range(2):
                        last = nc.tensor.matmul(
                            v_ps[:, t % V_SLOTS, tile, :],
                            w_st[:, k % W_SLOTS, tile, at * P:(at + 1) * P],
                            x_dup[:, blk % X_SLOTS, table, part, :],
                            start=(part == 0), stop=(part == 1))
                last.then_inc(v_done, 1)

            def reduce_batch(n):
                t0 = n * BATCH_STEPS
                chunk = t0 // ZSTEPS
                pe.wait_ge(prod_done, t0 + BATCH_STEPS)
                if t0 % ZSTEPS == 0 and chunk >= 1:
                    pe.wait_ge(z_high_done, chunk)
                    pe.wait_ge(z_low_done, chunk)
                tiles = min(ZTILES, 2 * NSTEPS - chunk * ZTILES)
                for i in range(2 * BATCH_STEPS):
                    step, tile = t0 + i // 2, 2 * t0 + i
                    quad = tile % 4
                    at = tile % ZTILES
                    dense_follows = quad == 0 and chunk == ZCHUNKS - 1
                    last = nc.tensor.matmul(z_ps[quad * QUAD:(quad + 1) * QUAD, :], selector_at(tile),
                                            prod[:, step % PROD_SLOTS, i % 2, :],
                                            start=(at < 4), stop=(at >= tiles - 4 and not dense_follows))
                if t0 == NSTEPS - BATCH_STEPS:
                    last = nc.tensor.matmul(z_ps[0:QUAD, :],
                                            ident[0:DENSE, QUAD - DENSE_ROW:2 * QUAD - DENSE_ROW],
                                            dense_sb[:, :], start=False, stop=True)
                last.then_inc(reduced, 1)

            for t in range(NSTEPS):
                for m in prep_block.get(t, []):
                    if m == LOOKED_UP[0]:
                        look_up_block(0, range(LOOKUP_CHUNKS))
                    elif m == LOOKED_UP[1]:
                        look_up_block(1, range(6, LOOKUP_CHUNKS))
                    else:
                        transpose_block(m)
                    if m == 1:
                        look_up_block(1, range(4))
                    if m == 2:
                        look_up_block(1, range(4, 6))
                bilinear(t)
                if t >= V_SLOTS and (t - V_SLOTS) % BATCH_STEPS == BATCH_STEPS - 1:
                    reduce_batch((t - V_SLOTS) // BATCH_STEPS)
            def layer1(i, chunks):
                cols = slice(i * P, (i + 1) * P)
                for n in chunks:
                    pe.wait_ge(z_high_done, n + 1)
                    pe.wait_ge(z_low_done, n + 1)
                    for p, (w, z) in enumerate(((w1_high, z_high), (w1_low, z_high), (w1_high, z_low))):
                        last = nc.tensor.matmul(h1_ps[i], w[:, n, cols], z[:, n, :], start=(n == 0 and p == 0),
                                                stop=(n == K1 - 1 and p == 2))
                if n == K1 - 1:
                    last.then_inc(h1_summed, 1)

            def layer2(i, chunks):
                cols = slice(i * P, (i + 1) * P)
                for n in chunks:
                    pe.wait_ge(h1_high_done, n + 1)
                    pe.wait_ge(h1_low_done, n + 1)
                    for p, (w, h) in enumerate(((w2_high, h1_high), (w2_low, h1_high), (w2_high, h1_low))):
                        last = nc.tensor.matmul(h2_ps[:, i, :], w[:, n, cols], h[:, n, :],
                                                start=(n == 0 and p == 0), stop=(n == K2 - 1 and p == 2))
                if n == K2 - 1:
                    last.then_inc(h2_summed, 1)

            pe.wait_ge(w1_high_done, K1)
            pe.wait_ge(w1_low_done, K1)
            pe.wait_ge(prod_done, NSTEPS - 2)
            layer1(0, range(K1 - 1))
            reduce_batch(NSTEPS // BATCH_STEPS - 1)
            layer1(1, range(K1 - 1))
            layer1(0, range(K1 - 1, K1))
            layer1(1, range(K1 - 1, K1))
            layer1(2, range(K1))
            layer1(3, range(K1))
            pe.wait_ge(w2_high_done, K2)
            pe.wait_ge(w2_low_done, K2)
            for chunks in (range(K2 - 1), range(K2 - 1, K2)):
                for i in range(K3):
                    layer2(i, chunks)
            pe.wait_ge(mlp_loaded, 48)
            pe.wait_ge(x_own_done, 4 * BLOCKS)
            pe.wait_ge(h2_done, K3)
            for k in range(ROWBLKS):
                for n in range(K3):
                    last = nc.tensor.matmul(y_ps[:, k:k + 1], h2[:, n, k * P:(k + 1) * P], w3_sb[:, n:n + 1],
                                            start=(n == 0), stop=(n == K3 - 1))
            last.then_inc(y_summed, 1)


def kernel(**inputs):
    import numpy as np
    import concourse.bacc as bacc
    from concourse.bass_utils import run_bass_kernel_spmd

    pair_of = {}
    for r in range(TABLES - 1):
        for c in range(r + 1, TABLES):
            pair_of[(r, c)] = len(pair_of)
    tiles = tile_pairs()

    table_at = table_order([inputs[f"tbl_{c}"].shape[0] for c in range(TABLES)])
    places = {a: i for i, a in enumerate(table_at)}
    assert sorted(places) == list(range(TABLES))

    def pair(rc):
        a, b = table_at[rc[0]], table_at[rc[1]]
        return pair_of[(min(a, b), max(a, b))], a > b

    param = np.asarray(inputs["L0_rec_param"]).transpose(1, 0, 2)
    npairs = param.shape[0]
    both_ways = np.concatenate([param, param.transpose(0, 2, 1), np.zeros((1, EMB, EMB), param.dtype)])
    order = np.array([[2 * npairs if rc is None else pair(rc)[0] + npairs * pair(rc)[1] for rc in t]
                      for t in tiles])
    weights = both_ways[order.reshape(NSTEPS, 2, 2)]
    weights = np.ascontiguousarray(weights.transpose(1, 3, 0, 2, 4).reshape(P, NSTEPS * P))

    w_top1 = np.asarray(inputs["W_top1"])
    w1 = np.zeros((ZCHUNKS * P, HID1), w_top1.dtype)
    for t, pairs in enumerate(tiles):
        for odd, rc in enumerate(pairs):
            if rc is not None:
                w1[z_row(t, odd)] = w_top1[pair(rc)[0]]
    dense_at = (ZCHUNKS - 1) * P + DENSE_ROW
    w1[dense_at:dense_at + DENSE] = w_top1[npairs:]

    consts = np.zeros((P, P + 4 * QUAD), np.float32)
    consts[:, QUAD:QUAD + P] = np.eye(P, dtype=np.float32)
    consts[0:EMB, P + 2 * QUAD + QUAD - 1] = 1.0
    consts[EMB:P, P + 2 * QUAD + QUAD] = 1.0

    arrays = {
        "dense_t": np.ascontiguousarray(np.asarray(inputs["dense_ctx"]).T),
        "ids": np.ascontiguousarray(np.asarray(inputs["ids"])[:, table_at]),
        "first_ids": np.ascontiguousarray(
            np.asarray(inputs["ids"]).T[[table_at[2 * m + i] for m in LOOKED_UP for i in range(2)]]),
        "weights": weights,
        "w1": w1,
        "b1": np.ascontiguousarray(np.asarray(inputs["b_top1"]).reshape(-1, P).T),
        "w2": np.ascontiguousarray(inputs["W_top2"]),
        "b2": np.ascontiguousarray(np.asarray(inputs["b_top2"]).reshape(-1, P).T),
        "w3": np.ascontiguousarray(np.asarray(inputs["W_top3"]).reshape(-1, P).T),
        "consts": consts,
        "row_numbers": np.arange(P * LOOKUP_CHUNKS, dtype=np.float32).reshape(P, LOOKUP_CHUNKS),
    }
    for c in range(TABLES):
        arrays[f"tbl_{c}"] = np.ascontiguousarray(inputs[f"tbl_{c}"])

    nc = bacc.Bacc("TRN2", target_bir_lowering=False, num_devices=1)
    dram = {name: nc.dram_tensor(name, a.shape, mybir.dt.from_np(a.dtype), kind="ExternalInput").ap()
            for name, a in arrays.items()}
    y = nc.dram_tensor("y", (P, ROWBLKS), F32, kind="ExternalOutput").ap()
    dlrm_tower(nc, dram["dense_t"], dram["ids"], dram["first_ids"], [dram[f"tbl_{c}"] for c in table_at],
               dram["weights"],
               dram["w1"], dram["b1"], dram["w2"], dram["b2"], dram["w3"], dram["consts"], dram["row_numbers"], y)
    result = run_bass_kernel_spmd(nc, [arrays], core_ids=[0])
    return result.results[0]["y"].T.reshape(BATCH, 1)
```
